# Optimizing a Trainium2 kernel written in Bass

```python
import numpy as np
import jax
import jax.numpy as jnp

def _softmax(x, axis=-1):
    return jax.nn.softmax(x, axis=axis)

def _gelu(x):
    return jax.nn.gelu(x, approximate=True)

def _silu(x):
    return jax.nn.silu(x)

def _sigmoid(x):
    return jax.nn.sigmoid(x)

def _layernorm(x, axis=-1, eps=1e-05):
    m = jnp.mean(x, axis=axis, keepdims=True)
    v = jnp.var(x, axis=axis, keepdims=True)
    return (x - m) / jnp.sqrt(v + eps)

def _scatter_add(tgt, idx, src, axis=0):
    return tgt.at[idx].add(src)

def _segment_sum(src, seg, n):
    return jax.ops.segment_sum(src, seg, n)
kernel_name = 'mk_adj_resnorm_d2_adj_r2_9c885a'

def setup_inputs(seed: int=0):
    np.random.seed(seed)
    _w = jnp.asarray

    def _rec_inputs():
        import jax
        import jax.numpy as jnp
        _gk = jax.random.key(seed)
        x = -0.0005207 + 1.001 * jax.random.normal(jax.random.fold_in(_gk, 1), (8192, 128), jnp.float32)
        _a = jax.random.bernoulli(jax.random.fold_in(_gk, 2), 0.000488281, (8192, 8192))
        _a = jnp.logical_or(_a, jnp.swapaxes(_a, -1, -2))
        _a = jnp.logical_or(_a, jnp.eye(8192, dtype=bool))
        _af = _a.astype(jnp.float32)
        _af = _af * jax.random.uniform(jax.random.fold_in(_gk, 3), (8192, 8192), jnp.float32, 0.05, 2.05)
        adj = _af
        return (x, adj)
    x, adj = _rec_inputs()

    def _L0_gnn_setup():
        import jax, jax.numpy as jnp
        import numpy as np
        N = 4096
        D = 128
        CUTOFF = 1.0
        MU = 1.0
        SIGMA = 0.5

        def sensitivity(r, mu, sigma):
            return jnp.exp(-(1.0 / r - 1.0 / mu) ** 2 / (2.0 * sigma * sigma))
        key = jax.random.key(seed)
        k_z, k_d, k_w = jax.random.split(key, 3)
        z = jax.random.normal(k_z, (N, D), dtype=jnp.float32)
        dist_matrix = jax.random.uniform(k_d, (N, N), dtype=jnp.float32) * 2.0 + 0.05
        W = jax.random.normal(k_w, (D, D), dtype=jnp.float32)
        B = jnp.zeros((D,), dtype=jnp.float32)
        return {'z': z, 'dist_matrix': dist_matrix, 'W': W, 'B': B}
    _L0_gnn_all = _L0_gnn_setup()
    _L0_gnn_in = {k: v for k, v in _L0_gnn_all.items() if k in ('W', 'B')}
    del _L0_gnn_all

    def _L1_gnn_setup():
        import jax, jax.numpy as jnp
        import numpy as np
        MIN_NORM = 1e-15
        BALL_EPS = 1e-05
        C_IN = 1.0
        C_OUT = 1.0

        def _artanh(x):
            x = jnp.clip(x, -1.0 + 1e-07, 1.0 - 1e-07)
            return 0.5 * (jnp.log1p(x) - jnp.log1p(-x))

        def _norm(x):
            return jnp.maximum(jnp.linalg.norm(x, axis=-1, keepdims=True), MIN_NORM)

        def proj(x, c):
            norm = _norm(x)
            maxnorm = (1.0 - BALL_EPS) / jnp.sqrt(c)
            return jnp.where(norm > maxnorm, x / norm * maxnorm, x)

        def expmap0(u, c):
            sc = jnp.sqrt(c)
            un = _norm(u)
            return jnp.tanh(sc * un) * u / (sc * un)

        def logmap0(p, c):
            sc = jnp.sqrt(c)
            pn = _norm(p)
            return _artanh(sc * pn) * p / (sc * pn)

        def mobius_matvec(m, x, c):
            sc = jnp.sqrt(c)
            xn = _norm(x)
            mx = x @ m.T
            mxn = _norm(mx)
            res = jnp.tanh(mxn / xn * _artanh(sc * xn)) * mx / (mxn * sc)
            zero_row = jnp.all(mx == 0, axis=-1, keepdims=True)
            return jnp.where(zero_row, jnp.zeros((), dtype=res.dtype), res)

        def mobius_add(x, y, c):
            x2 = jnp.sum(x * x, axis=-1, keepdims=True)
            y2 = jnp.sum(y * y, axis=-1, keepdims=True)
            xy = jnp.sum(x * y, axis=-1, keepdims=True)
            num = (1.0 + 2.0 * c * xy + c * y2) * x + (1.0 - c * x2) * y
            denom = 1.0 + 2.0 * c * xy + c * c * x2 * y2
            return num / jnp.maximum(denom, MIN_NORM)
        key = jax.random.key(seed)
        k1, k2, k3, k4 = jax.random.split(key, 4)
        N, D_IN, D_OUT = (4096, 128, 128)
        x = proj(0.05 * jax.random.normal(k1, (N, D_IN), dtype=jnp.float32), C_IN)
        adj = jax.random.uniform(k2, (N, N), dtype=jnp.float32)
        adj = adj / jnp.sum(adj, axis=1, keepdims=True)
        bound = np.sqrt(2.0) * np.sqrt(6.0 / (D_IN + D_OUT))
        weight = jax.random.uniform(k3, (D_OUT, D_IN), dtype=jnp.float32, minval=-bound, maxval=bound)
        bias = 0.01 * jax.random.normal(k4, (D_OUT,), dtype=jnp.float32)
        return {'x': x, 'adj': adj, 'weight': weight, 'bias': bias}
    _L1_gnn_all = _L1_gnn_setup()
    _L1_gnn_in = {k: v for k, v in _L1_gnn_all.items() if k in ('weight', 'bias')}
    del _L1_gnn_all
    return {'x': x, 'adj': adj, 'L0_gnn_W': _L0_gnn_in['W'], 'L0_gnn_B': _L0_gnn_in['B'], 'L1_gnn_weight': _L1_gnn_in['weight'], 'L1_gnn_bias': _L1_gnn_in['bias']}

def reference(x, adj, L0_gnn_W, L0_gnn_B, L1_gnn_weight, L1_gnn_bias):
    import jax
    import jax.numpy as jnp

    def _L0_gnn_ref(z, dist_matrix, W, B):
        import jax, jax.numpy as jnp
        import numpy as np
        N = 4096
        D = 128
        CUTOFF = 1.0
        MU = 1.0
        SIGMA = 0.5

        def sensitivity(r, mu, sigma):
            return jnp.exp(-(1.0 / r - 1.0 / mu) ** 2 / (2.0 * sigma * sigma))
        msg = z @ W + B
        sens = sensitivity(dist_matrix, MU, SIGMA)
        weights = jnp.where(dist_matrix < CUTOFF, sens, 0.0)
        return weights @ msg

    def _L1_gnn_ref(x, adj, weight, bias):
        import jax, jax.numpy as jnp
        import numpy as np
        MIN_NORM = 1e-15
        BALL_EPS = 1e-05
        C_IN = 1.0
        C_OUT = 1.0

        def _artanh(x):
            x = jnp.clip(x, -1.0 + 1e-07, 1.0 - 1e-07)
            return 0.5 * (jnp.log1p(x) - jnp.log1p(-x))

        def _norm(x):
            return jnp.maximum(jnp.linalg.norm(x, axis=-1, keepdims=True), MIN_NORM)

        def proj(x, c):
            norm = _norm(x)
            maxnorm = (1.0 - BALL_EPS) / jnp.sqrt(c)
            return jnp.where(norm > maxnorm, x / norm * maxnorm, x)

        def expmap0(u, c):
            sc = jnp.sqrt(c)
            un = _norm(u)
            return jnp.tanh(sc * un) * u / (sc * un)

        def logmap0(p, c):
            sc = jnp.sqrt(c)
            pn = _norm(p)
            return _artanh(sc * pn) * p / (sc * pn)

        def mobius_matvec(m, x, c):
            sc = jnp.sqrt(c)
            xn = _norm(x)
            mx = x @ m.T
            mxn = _norm(mx)
            res = jnp.tanh(mxn / xn * _artanh(sc * xn)) * mx / (mxn * sc)
            zero_row = jnp.all(mx == 0, axis=-1, keepdims=True)
            return jnp.where(zero_row, jnp.zeros((), dtype=res.dtype), res)

        def mobius_add(x, y, c):
            x2 = jnp.sum(x * x, axis=-1, keepdims=True)
            y2 = jnp.sum(y * y, axis=-1, keepdims=True)
            xy = jnp.sum(x * y, axis=-1, keepdims=True)
            num = (1.0 + 2.0 * c * xy + c * y2) * x + (1.0 - c * x2) * y
            denom = 1.0 + 2.0 * c * xy + c * c * x2 * y2
            return num / jnp.maximum(denom, MIN_NORM)
        h = proj(mobius_matvec(weight, x, C_IN), C_IN)
        hyp_bias = proj(expmap0(bias[None, :], C_IN), C_IN)
        h = proj(mobius_add(h, hyp_bias, C_IN), C_IN)
        x_tangent = logmap0(h, C_IN)
        support_t = adj @ x_tangent
        h = proj(expmap0(support_t, C_IN), C_IN)
        xt = jax.nn.relu(logmap0(h, C_IN))
        return proj(expmap0(xt, C_OUT), C_OUT)
    x = _layernorm(x + _L0_gnn_ref(x, adj, L0_gnn_W, L0_gnn_B), axis=-1)
    x = _layernorm(x + _L1_gnn_ref(x, adj, L1_gnn_weight, L1_gnn_bias), axis=-1)
    return x

_drawn_inputs = setup_inputs


def setup_inputs(seed=0):
    import zlib

    import numpy as np

    out = dict(_drawn_inputs(seed))
    spreads = {'L0_gnn_B': (0.0, 0.655)}
    factors = {'L1_gnn_bias': 8.0}
    for name, (base, spread) in spreads.items():
        noise = np.random.default_rng([zlib.crc32(name.encode()), seed]).standard_normal(out[name].shape)
        drawn = base * np.exp(spread * noise) if base else spread * noise
        out[name] = jnp.asarray(drawn.astype(out[name].dtype))
    for name, factor in factors.items():
        out[name] = (out[name] * factor).astype(out[name].dtype)
    return out
```

```python
from contextlib import ExitStack

import concourse.bass as bass
import numpy as np
from concourse import mybir

P = 128
N = 8192
BLK = 512
NB = N // BLK
T = BLK // P
NA = 8
NX = 4

LN_EPS = 1e-5
MIN_NORM2 = 1e-30
BALL = float(np.float32(1.0 - 1e-5))
ART_MAX = float(np.float32(1.0 - 1e-7))
BALL_GAP = (1.0 - BALL) * (1.0 + BALL)
ART_BALL = float(np.arctanh(np.float64(BALL)))
TINY_R = 1e-18

PRE_LINKS = 8
LIFT_LINKS = 36
LAND_LINKS = 22


def gnn_kernel(nc, x, x_cols, adj, w0, b0, w1, w1_cols, b1, eye, x1_dram, out):
    f32 = mybir.dt.float32
    ALU = mybir.AluOpType
    ACT = mybir.ActivationFunctionType
    AX = mybir.AxisListType.X

    x_blocks = x.rearrange("(n t p) f -> n p t f", t=T, p=P)
    x1_blocks = x1_dram.rearrange("(n t p) f -> n p t f", t=T, p=P)
    out_blocks = out.rearrange("(n t p) f -> n p t f", t=T, p=P)

    with ExitStack() as ctx:
        def sb(name, shape):
            return ctx.enter_context(nc.sbuf_tensor(name, shape, f32))

        def pb(name, shape):
            return ctx.enter_context(nc.psum_tensor(name, shape, f32))

        def sem(name):
            return ctx.enter_context(nc.semaphore(name))

        msg = sb("msg", [P, NB, T, P])
        tan = sb("tan", [P, NB, T, P])
        x_col = tan[:, :, :, :].rearrange("p n t f -> p (n t f)")
        pair = [sb(f"pair{i}", [P, T, BLK]) for i in range(NA)]
        wt = [sb(f"wt{i}", [P, T, BLK]) for i in range(NX)]
        o_t = sb("o_t", [P, T, P])
        x_in = sb("x_in", [P, T, P])
        row = sb("row", [P, T, P])
        x1_t = sb("x1_t", [P, T, P])
        mx = sb("mx", [P, T, P])
        sq = sb("sq", [P, T, P])
        w0_sb = sb("w0_sb", [P, P])
        b0_sb = sb("b0_sb", [P, P])
        w1_sb = sb("w1_sb", [P, P])
        w1c_sb = sb("w1c_sb", [P, P])
        b1_sb = sb("b1_sb", [P, P])
        hb = sb("hb", [P, P])
        hb_col = sb("hb_col", [P, 1])
        wb = sb("wb", [P, 1])
        eye_sb = sb("eye_sb", [P, P])
        c = sb("c", [P, 16])
        s = sb("s", [P, 32, T])

        acc0 = [pb(f"acc0_{i}", [P, BLK]) for i in range(2)]
        acc1 = [pb(f"acc1_{i}", [P, BLK]) for i in range(2)]
        turned = pb("turned", [P, T, P])
        mx_ps = pb("mx_ps", [P, T, P])
        xb_ps = pb("xb_ps", [P, T])

        small_loaded = sem("small_loaded")
        eye_loaded = sem("eye_loaded")
        xcol_loaded = [sem(f"xcol_loaded{i}") for i in range(4)]
        adj_loaded = [sem(f"adj_loaded{i}") for i in range(NA)]
        xin_loaded = sem("xin_loaded")
        x1_stored = sem("x1_stored")
        out_stored = sem("out_stored")
        bias_sq = sem("bias_sq")
        bias_exp = sem("bias_exp")
        hb_ready = sem("hb_ready")
        hb_turned = sem("hb_turned")
        hbcol_ready = sem("hbcol_ready")
        wb_done = sem("wb_done")
        wb_ready = sem("wb_ready")
        msg_done = sem("msg_done")
        msg_ready = sem("msg_ready")
        ln_ready = sem("ln_ready")
        inv_ready = sem("inv_ready")
        z_ready = sem("z_ready")
        e_ready = sem("e_ready")
        w_ready = sem("w_ready")
        l0_done = sem("l0_done")
        l1_done = sem("l1_done")
        consts_ready = sem("consts_ready")
        act_ln = sem("act_ln")
        dve_step = sem("dve_step")
        act_step = sem("act_step")
        o_ready = sem("o_ready")
        o_turned = sem("o_turned")
        var_ready = sem("var_ready")
        rstd_ready = sem("rstd_ready")
        x1_ready = sem("x1_ready")
        x1_turned = sem("x1_turned")
        x1t_ready = sem("x1t_ready")
        mx_done = sem("mx_done")
        norms_ready = sem("norms_ready")
        roots_ready = sem("roots_ready")
        clip_ready = sem("clip_ready")
        art_ready = sem("art_ready")
        arg_ready = sem("arg_ready")
        tanh_ready = sem("tanh_ready")
        sum_ready = sem("sum_ready")
        sumroot_ready = sem("sumroot_ready")
        sumclip_ready = sem("sumclip_ready")
        sumart_ready = sem("sumart_ready")
        tan_ready = sem("tan_ready")
        y_o_ready = sem("y_o_ready")
        y_o_turned = sem("y_o_turned")
        y_norms_ready = sem("y_norms_ready")
        y_roots_ready = sem("y_roots_ready")
        y_arg_ready = sem("y_arg_ready")
        y_tanh_ready = sem("y_tanh_ready")
        y_var_ready = sem("y_var_ready")
        y_rstd_ready = sem("y_rstd_ready")
        y_ready = sem("y_ready")
        y_xin_loaded = sem("y_xin_loaded")

        block = ctx.enter_context(nc.Block())

        def q(k, n=1):
            return s[:, k:k + n, :]

        def wide(k):
            return s[:, k, :].unsqueeze(2).to_broadcast([P, T, P])

        @block.sync
        def _(sp):
            def load(i, n_before, b):
                k = b % NA
                sp.dma_start(pair[k][:, :, :], adj[i, b]).then_inc(adj_loaded[k], 16)

            for dst, src in ((w0_sb, w0), (b0_sb, b0), (b1_sb, b1)):
                sp.dma_start(dst[:, :], src).then_inc(small_loaded, 16)
            for i in range(4):
                cols = slice(i * N // 4, (i + 1) * N // 4)
                sp.dma_start(x_col[:, cols], x_cols[:, cols]).then_inc(xcol_loaded[i], 16)
                if i < 2:
                    load(0, 0, i)
            for dst, src in ((w1_sb, w1), (w1c_sb, w1_cols), (eye_sb, eye)):
                sp.dma_start(dst[:, :], src).then_inc(eye_loaded, 16)
            for b in range(2, NB):
                if b >= NA:
                    sp.wait_ge(w_ready, b - NA + 1)
                load(0, 0, b)
            with sp.Fori(1, NB) as i:
                for b in range(NB):
                    sp.wait_ge(w_ready, i * NB + (b - NA + 1))
                    load(i, i * NB, b)
            for b in range(NB):
                if b < NA:
                    sp.wait_ge(w_ready, NB * NB + b - NA + 1)
                else:
                    sp.wait_ge(l1_done, b - NA + 1)
                load(0, NB * NB, b)
            with sp.Fori(1, NB) as i:
                for b in range(NB):
                    sp.wait_ge(l1_done, i * NB + (b - NA + 1))
                    load(i, i * NB, b)

        @block.gpsimd
        def _(pool):
            pool.dma_start(x_in[:, :, :], x_blocks[0]).then_inc(xin_loaded, 16)

            def store_x1(i):
                pool.wait_ge(x1_ready, i + 1)
                pool.dma_start(x1_blocks[i], row[:, :, :]).then_inc(x1_stored, 16)
                pool.wait_ge(x1_stored, (i + 1) * 16)

            with pool.Fori(0, NB - 1) as i:
                store_x1(i)
                pool.dma_start(x_in[:, :, :], x_blocks[i + 1]).then_inc(xin_loaded, 16)
            store_x1(NB - 1)
            pool.dma_start(x_in[:, :, :], x1_blocks[0]).then_inc(y_xin_loaded, 16)

            def store_y(i):
                pool.wait_ge(y_ready, i + 1)
                pool.dma_start(out_blocks[i], row[:, :, :]).then_inc(out_stored, 16)
                pool.wait_ge(out_stored, (i + 1) * 16)

            with pool.Fori(0, NB - 1) as i:
                store_y(i)
                pool.dma_start(x_in[:, :, :], x1_blocks[i + 1]).then_inc(y_xin_loaded, 16)
            store_y(NB - 1)

        @block.scalar
        def _(act):
            nc.scalar.preload_act_table_set("natural_log_exp_and_others")

            def chained(ins, count):
                ins.then_inc(act_step, 1)
                act.wait_ge(act_step, count)

            act.wait_ge(bias_sq, 1)
            chained(nc.scalar.activation(c[:, 1:2], c[:, 0:1], ACT.Ln), 1)
            nc.scalar.activation(c[:, 2:3], c[:, 1:2], ACT.Exp, scale=-0.5)
            chained(nc.scalar.activation(c[:, 3:4], c[:, 1:2], ACT.Exp, scale=0.5), 2)
            nc.scalar.activation(c[:, 4:5], c[:, 3:4], ACT.Exp, scale=-2.0).then_inc(bias_exp, 1)

            def logs(i, b):
                k = b % NA
                act.wait_ge(adj_loaded[k], (i * (NB // NA) + (b // NA + 1)) * 16)
                if not (isinstance(i, int) and i * NB + b < NX):
                    act.wait_ge(l0_done, i * NB + (b - NX + 1))
                nc.scalar.activation(wt[b % NX][:, :, :], pair[k][:, :, :], ACT.Ln,
                                     bias=c[:, 15:16]).then_inc(ln_ready, 1)

            def inverses(i, b):
                act.wait_ge(ln_ready, i * NB + (b + 1))
                nc.scalar.activation(wt[b % NX][:, :, :], wt[b % NX][:, :, :], ACT.Exp,
                                     scale=-2.0).then_inc(inv_ready, 1)

            def exps(i, b):
                act.wait_ge(z_ready, i * NB + (b + 1))
                nc.scalar.activation(wt[b % NX][:, :, :], wt[b % NX][:, :, :], ACT.Exp,
                                     bias=c[:, 14:15], scale=4.0).then_inc(e_ready, 1)

            def lift(i, b):
                if b == 3:
                    act.wait_ge(var_ready, i + 1)
                    chained(nc.scalar.activation(q(1), q(0), ACT.Ln, scale=1.0 / P, bias=c[:, 13:14]), i * 2 + 3)
                    nc.scalar.activation(q(2), q(1), ACT.Exp, scale=-0.5).then_inc(rstd_ready, 1)
                if b == 9:
                    act.wait_ge(norms_ready, i + 1)
                    chained(nc.scalar.activation(q(6, 2), q(4, 2), ACT.Ln), i * 2 + 4)
                    nc.scalar.activation(q(8), q(6), ACT.Exp, scale=0.5)
                    nc.scalar.activation(q(9), q(7), ACT.Exp, scale=-0.5).then_inc(roots_ready, 1)
                if b == 10:
                    act.wait_ge(clip_ready, i + 1)
                    nc.scalar.activation(q(12), q(10), ACT.Ln, bias=1.0)
                    nc.scalar.activation(q(13), q(10), ACT.Ln, scale=-1.0, bias=1.0)
                    nc.scalar.activation(q(14), q(11), ACT.Exp, scale=0.5).then_inc(art_ready, 1)
                if b == 11:
                    act.wait_ge(arg_ready, i + 1)
                    nc.scalar.activation(q(16), q(15), ACT.Exp, scale=-1.0).then_inc(tanh_ready, 1)
                if b == 12:
                    act.wait_ge(sum_ready, i + 1)
                    nc.scalar.activation(q(24), q(23), ACT.Ln).then_inc(act_ln, 1)
                    act.wait_ge(act_ln, i + 1)
                    nc.scalar.activation(q(25), q(24), ACT.Exp, scale=0.5)
                    nc.scalar.activation(q(26), q(24), ACT.Exp, scale=-0.5).then_inc(sumroot_ready, 1)
                if b == 13:
                    act.wait_ge(sumclip_ready, i + 1)
                    nc.scalar.activation(q(28), q(27), ACT.Ln, bias=1.0)
                    nc.scalar.activation(q(29), q(22), ACT.Ln).then_inc(sumart_ready, 1)

            def step(i, first=False, last=False):
                for b in range(NB):
                    ahead = not (last and b + 2 >= NB)
                    if ahead:
                        logs(i, b + 2)
                    exps(i, b)
                    if ahead:
                        inverses(i, b + 2)
                    if not first:
                        lift(i - 1, b)

            act.wait_ge(consts_ready, 1)
            for b in range(2):
                logs(0, b)
                inverses(0, b)
            step(0, first=True)
            with act.Fori(1, NB - 1) as i:
                step(i)
            step(NB - 1, last=True)
            for b in range(NB):
                lift(NB - 1, b)

            def land(i):
                act.wait_ge(y_norms_ready, i + 1)
                chained(nc.scalar.activation(q(6, 2), q(4, 2), ACT.Ln), i * 2 + 3 + 2 * NB)
                nc.scalar.activation(q(8), q(6), ACT.Exp, scale=0.5)
                nc.scalar.activation(q(9), q(6), ACT.Exp, scale=-0.5)
                nc.scalar.activation(q(10), q(7), ACT.Exp, scale=0.5)
                nc.scalar.activation(q(11), q(7), ACT.Exp, scale=-0.5).then_inc(y_roots_ready, 1)
                act.wait_ge(y_arg_ready, i + 1)
                nc.scalar.activation(q(13), q(12), ACT.Exp, scale=-2.0).then_inc(y_tanh_ready, 1)
                act.wait_ge(y_var_ready, i + 1)
                chained(nc.scalar.activation(q(1), q(0), ACT.Ln, scale=1.0 / P, bias=c[:, 13:14]),
                        i * 2 + 4 + 2 * NB)
                nc.scalar.activation(q(2), q(1), ACT.Exp, scale=-0.5).then_inc(y_rstd_ready, 1)

            with act.Fori(0, NB) as i:
                land(i)

        @block.vector
        def _(dve):
            v = nc.vector
            state = {"base": 0, "count": 0}

            def link(ins):
                state["count"] += 1
                ins.then_inc(dve_step, 1)
                dve.wait_ge(dve_step, state["base"] + state["count"])

            def links(base, count, body):
                state["base"], state["count"] = base, 0
                body()
                assert state["count"] == count, state["count"]

            def pre():
                v.memset(c[:, 15:16], TINY_R)
                v.memset(c[:, 14:15], -2.0)
                v.memset(c[:, 13:14], LN_EPS).then_inc(consts_ready, 1)
                dve.wait_ge(small_loaded, 48)
                link(v.tensor_tensor(hb[:, :], b1_sb[:, :], b1_sb[:, :], ALU.mult))
                link(v.tensor_reduce(c[:, 5:6], hb[:, :], AX, ALU.add))
                v.tensor_scalar(c[:, 0:1], c[:, 5:6], MIN_NORM2, None, ALU.max).then_inc(bias_sq, 1)
                dve.wait_ge(bias_exp, 1)
                v.tensor_scalar(c[:, 6:7], c[:, 4:5], -1.0, 1.0, ALU.mult, ALU.add)
                link(v.tensor_scalar(c[:, 7:8], c[:, 4:5], 1.0, None, ALU.add))
                link(v.reciprocal(c[:, 8:9], c[:, 7:8]))
                link(v.tensor_scalar(c[:, 9:10], c[:, 6:7], c[:, 8:9], BALL, ALU.mult, ALU.min))
                v.tensor_scalar(hb[:, :], b1_sb[:, :], c[:, 9:10], c[:, 2:3], ALU.mult, ALU.mult).then_inc(hb_ready, 1)
                v.tensor_scalar(c[:, 5:6], c[:, 9:10], -1.0, 1.0, ALU.mult, ALU.add)
                link(v.tensor_tensor(c[:, 10:11], c[:, 9:10], c[:, 9:10], ALU.mult))
                v.tensor_scalar(c[:, 11:12], c[:, 10:11], 1.0, None, ALU.add)
                v.tensor_scalar(c[:, 12:13], c[:, 10:11], -1.0, None, ALU.mult)
                link(v.tensor_scalar(c[:, 6:7], c[:, 9:10], 1.0, None, ALU.add))
                link(v.tensor_tensor(c[:, 3:4], c[:, 5:6], c[:, 6:7], ALU.mult))
                dve.wait_ge(hb_turned, 1)
                v.tensor_copy(hb_col[:, :], turned[:, 0, 0:1]).then_inc(hbcol_ready, 1)
                dve.wait_ge(wb_done, 1)
                v.tensor_copy(wb[:, :], xb_ps[:, 0:1]).then_inc(wb_ready, 1)

            links(0, PRE_LINKS, pre)

            def messages(b):
                dve.wait_ge(msg_done, b + 1)
                v.tensor_tensor(msg[:, b, :, :], acc1[b % 2][:, :].rearrange("p (t f) -> p t f", t=T),
                                b0_sb[:, :].unsqueeze(1).to_broadcast([P, T, P]), ALU.add).then_inc(msg_ready, 1)

            def halves(i, b):
                buf = wt[b % NX][:, :, :]
                dve.wait_ge(inv_ready, i * NB + (b + 1))
                v.scalar_tensor_tensor(buf, pair[b % NA][:, :, :], 0.5, buf, ALU.subtract, ALU.mult).then_inc(z_ready, 1)

            def masks(i, b):
                buf = wt[b % NX][:, :, :]
                dve.wait_ge(e_ready, i * NB + (b + 1))
                v.scalar_tensor_tensor(buf, pair[b % NA][:, :, :], 1.0, buf, ALU.is_lt, ALU.mult).then_inc(w_ready, 1)

            def deviations():
                link(v.tensor_reduce(q(3), row[:, :, :], AX, ALU.add))
                link(v.tensor_scalar(q(1), q(3), -1.0 / P, None, ALU.mult))
                link(v.tensor_tensor(row[:, :, :], row[:, :, :], wide(1), ALU.add))
                link(v.tensor_tensor(sq[:, :, :], row[:, :, :], row[:, :, :], ALU.mult))
                return v.tensor_reduce(q(0), sq[:, :, :], AX, ALU.add)

            def refined_rstd():
                v.tensor_scalar(q(30), q(0), 1.0 / P, LN_EPS, ALU.mult, ALU.add)
                link(v.tensor_tensor(q(31), q(2), q(2), ALU.mult))
                link(v.tensor_tensor(q(30), q(30), q(31), ALU.mult))
                link(v.tensor_scalar(q(31), q(30), -0.5, 1.5, ALU.mult, ALU.add))
                link(v.tensor_tensor(q(3), q(2), q(31), ALU.mult))

            def lift(i, b):
                if b == 0:
                    dve.wait_ge(l0_done, (i + 1) * NB)
                    v.tensor_copy(o_t[:, :, :].rearrange("p t f -> p (t f)"), acc0_of(i)).then_inc(o_ready, 1)
                if b == 2:
                    dve.wait_ge(o_turned, i + 1)
                    dve.wait_ge(xin_loaded, (i + 1) * 16)
                    link(v.tensor_tensor(row[:, :, :], turned[:, :, :], x_in[:, :, :], ALU.add))
                    deviations().then_inc(var_ready, 1)
                if b == 4:
                    dve.wait_ge(rstd_ready, i + 1)
                    refined_rstd()
                    v.tensor_tensor(row[:, :, :], row[:, :, :], wide(3), ALU.mult).then_inc(x1_ready, 1)
                    link(v.tensor_tensor(q(30), q(0), q(3), ALU.mult))
                    link(v.tensor_tensor(q(31), q(30), q(3), ALU.mult))
                    link(v.tensor_scalar(q(4), q(31), MIN_NORM2, None, ALU.max))
                if b == 6:
                    dve.wait_ge(x1_turned, i + 1)
                    v.tensor_copy(x1_t[:, :, :], turned[:, :, :]).then_inc(x1t_ready, 1)
                if b == 8:
                    dve.wait_ge(mx_done, i + 1)
                    v.tensor_copy(q(17), xb_ps[:, :].unsqueeze(1))
                    link(v.tensor_copy(mx[:, :, :], mx_ps[:, :, :]))
                    link(v.tensor_tensor(sq[:, :, :], mx[:, :, :], mx[:, :, :], ALU.mult))
                    link(v.tensor_reduce(q(31), sq[:, :, :], AX, ALU.add))
                    v.tensor_scalar(q(5), q(31), MIN_NORM2, None, ALU.max).then_inc(norms_ready, 1)
                if b == 9:
                    dve.wait_ge(roots_ready, i + 1)
                    v.tensor_scalar(q(10), q(8), ART_MAX, None, ALU.min)
                    v.tensor_tensor(q(11), q(7), q(6), ALU.subtract).then_inc(clip_ready, 1)
                if b == 10:
                    dve.wait_ge(art_ready, i + 1)
                    link(v.tensor_tensor(q(15), q(12), q(13), ALU.subtract))
                    v.tensor_tensor(q(15), q(15), q(14), ALU.mult).then_inc(arg_ready, 1)
                if b == 11:
                    dve.wait_ge(tanh_ready, i + 1)
                    v.tensor_scalar(q(18), q(16), -1.0, 1.0, ALU.mult, ALU.add)
                    link(v.tensor_scalar(q(19), q(16), 1.0, None, ALU.add))
                    link(v.reciprocal(q(20), q(19)))
                    link(v.tensor_tensor(q(18), q(18), q(20), ALU.mult))
                    link(v.tensor_scalar(q(18), q(18), BALL, None, ALU.min))
                    v.tensor_scalar(q(20), q(18), -1.0, 1.0, ALU.mult, ALU.add)
                    v.tensor_scalar(q(21), q(18), 1.0, None, ALU.add)
                    link(v.tensor_tensor(q(19), q(18), q(9), ALU.mult))
                    v.tensor_tensor(q(20), q(20), q(21), ALU.mult)
                    link(v.tensor_tensor(q(17), q(17), q(19), ALU.mult))
                    link(v.tensor_scalar(q(21), q(17), 2.0, c[:, 11:12], ALU.mult, ALU.add))
                    link(v.scalar_tensor_tensor(q(22), q(20), c[:, 12:13], q(21), ALU.mult, ALU.add))
                    link(v.tensor_scalar(q(22), q(22), 1e-15, None, ALU.max))
                    link(v.reciprocal(q(30), q(22)))
                    link(v.tensor_tensor(q(31), q(20), q(30), ALU.mult))
                    link(v.tensor_scalar(q(31), q(31), c[:, 3:4], None, ALU.mult))
                    link(v.tensor_scalar(q(22), q(31), BALL_GAP, None, ALU.max))
                    link(v.tensor_scalar(q(23), q(31), -1.0, 1.0, ALU.mult, ALU.add))
                    v.tensor_scalar(q(23), q(23), MIN_NORM2, None, ALU.max).then_inc(sum_ready, 1)
                if b == 12:
                    dve.wait_ge(sumroot_ready, i + 1)
                    v.tensor_scalar(q(27), q(25), BALL, None, ALU.min).then_inc(sumclip_ready, 1)
                    link(v.tensor_tensor(q(24), q(26), q(30), ALU.mult))
                if b == 13:
                    dve.wait_ge(sumart_ready, i + 1)
                    link(v.scalar_tensor_tensor(q(31), q(29), -0.5, q(28), ALU.mult, ALU.add))
                    link(v.tensor_tensor(q(31), q(31), q(24), ALU.mult))
                    v.tensor_tensor(q(21), q(21), q(19), ALU.mult)
                    link(v.tensor_tensor(q(23), q(20), q(31), ALU.mult))
                    link(v.tensor_tensor(q(22), q(21), q(31), ALU.mult))
                if b == 14:
                    hb_wide = hb[:, :].unsqueeze(1).to_broadcast([P, T, P])
                    v.tensor_tensor(mx[:, :, :], mx[:, :, :], wide(22), ALU.mult)
                    link(v.tensor_tensor(sq[:, :, :], hb_wide, wide(23), ALU.mult))
                    v.tensor_tensor(tan[:, i, :, :], mx[:, :, :], sq[:, :, :], ALU.add).then_inc(tan_ready, 1)

            lift_marks = {"acc": None}

            def acc0_of(i):
                return acc0[lift_marks["acc"]][:, :]

            def step(i, odd, first=False, last=False):
                lift_marks["acc"] = 1 - odd

                def body():
                    for b in range(NB):
                        if first:
                            messages(b)
                        if not (last and b + 1 >= NB):
                            halves(i, b + 1)
                        masks(i, b)
                        if not first:
                            lift(i - 1, b)

                links(PRE_LINKS + (i - 1) * LIFT_LINKS, 0 if first else LIFT_LINKS, body)

            halves(0, 0)
            step(0, 0, first=True)
            with dve.Fori(1, NB - 1, 2) as i:
                step(i, 1)
                step(i + 1, 0)
            step(NB - 1, 1, last=True)
            lift_marks["acc"] = 1
            links(PRE_LINKS + (NB - 1) * LIFT_LINKS, LIFT_LINKS,
                  lambda: [lift(NB - 1, b) for b in range(NB)])

            def land(i, odd):
                dve.wait_ge(l1_done, (i + 1) * NB)
                v.tensor_copy(o_t[:, :, :].rearrange("p t f -> p (t f)"), acc1[odd][:, :]).then_inc(y_o_ready, 1)
                dve.wait_ge(y_o_turned, i + 1)
                link(v.tensor_copy(mx[:, :, :], turned[:, :, :]))
                v.tensor_scalar(x1_t[:, :, :], mx[:, :, :], 0.0, None, ALU.max)
                link(v.tensor_tensor(sq[:, :, :], mx[:, :, :], mx[:, :, :], ALU.mult))
                link(v.tensor_reduce(q(30), sq[:, :, :], AX, ALU.add))
                link(v.tensor_tensor(sq[:, :, :], x1_t[:, :, :], x1_t[:, :, :], ALU.mult))
                link(v.tensor_reduce(q(31), sq[:, :, :], AX, ALU.add))
                v.tensor_scalar(q(4, 2), q(30, 2), MIN_NORM2, None, ALU.max).then_inc(y_norms_ready, 1)
                dve.wait_ge(y_roots_ready, i + 1)
                link(v.tensor_scalar(q(12), q(8), ART_BALL, None, ALU.min))
                link(v.tensor_tensor(q(14), q(12), q(9), ALU.mult))
                v.tensor_tensor(q(12), q(14), q(10), ALU.mult).then_inc(y_arg_ready, 1)
                dve.wait_ge(y_tanh_ready, i + 1)
                v.tensor_scalar(q(15), q(13), -1.0, 1.0, ALU.mult, ALU.add)
                link(v.tensor_scalar(q(16), q(13), 1.0, None, ALU.add))
                link(v.reciprocal(q(17), q(16)))
                link(v.tensor_tensor(q(15), q(15), q(17), ALU.mult))
                link(v.tensor_scalar(q(15), q(15), BALL, None, ALU.min))
                link(v.tensor_tensor(q(18), q(15), q(11), ALU.mult))
                link(v.tensor_tensor(x1_t[:, :, :], x1_t[:, :, :], wide(18), ALU.mult))
                dve.wait_ge(y_xin_loaded, (i + 1) * 16)
                link(v.tensor_tensor(row[:, :, :], x1_t[:, :, :], x_in[:, :, :], ALU.add))
                deviations().then_inc(y_var_ready, 1)
                dve.wait_ge(y_rstd_ready, i + 1)
                refined_rstd()
                v.tensor_tensor(row[:, :, :], row[:, :, :], wide(3), ALU.mult).then_inc(y_ready, 1)

            def land_step(i, odd):
                links(PRE_LINKS + NB * LIFT_LINKS + i * LAND_LINKS, LAND_LINKS, lambda: land(i, odd))

            land_step(0, 0)
            with dve.Fori(1, NB - 1, 2) as i:
                land_step(i, 1)
                land_step(i + 1, 0)
            land_step(NB - 1, 1)

        @block.tensor
        def _(pe):
            mm = nc.tensor.matmul

            pe.wait_ge(eye_loaded, 48)
            pe.wait_ge(hb_ready, 1)
            nc.tensor.transpose(turned[:, 0, :], hb[:, :], eye_sb[:, :]).then_inc(hb_turned, 1)
            pe.wait_ge(hbcol_ready, 1)
            mm(xb_ps[:, 0:1], w1_sb[:, :], hb_col[:, :], start=True, stop=True).then_inc(wb_done, 1)

            def messages(b):
                if b % 4 == 0:
                    pe.wait_ge(xcol_loaded[b // 4], 16)
                if b >= 2:
                    pe.wait_ge(msg_ready, b - 1)
                for t in range(T):
                    col = (b * T + t) * P
                    last = mm(acc1[b % 2][:, t * P:(t + 1) * P], x_col[:, col:col + P], w0_sb[:, :],
                              start=True, stop=True)
                last.then_inc(msg_done, 1)

            def layer0(i, b, odd, first):
                if first:
                    pe.wait_ge(msg_ready, b + 1)
                pe.wait_ge(w_ready, i * NB + (b + 1))
                for t in range(T):
                    last = mm(acc0[odd][:, :], msg[:, b, t, :], wt[b % NX][:, t, :],
                              start=(b == 0 and t == 0), stop=(b == NB - 1 and t == T - 1))
                last.then_inc(l0_done, 1)

            def lift(i, b):
                if b == 1:
                    pe.wait_ge(o_ready, i + 1)
                    for t in range(T):
                        last = nc.tensor.transpose(turned[:, t, :], o_t[:, t, :], eye_sb[:, :])
                    last.then_inc(o_turned, 1)
                if b == 5:
                    pe.wait_ge(x1_ready, i + 1)
                    for t in range(T):
                        last = nc.tensor.transpose(turned[:, t, :], row[:, t, :], eye_sb[:, :])
                    last.then_inc(x1_turned, 1)
                if b == 7:
                    pe.wait_ge(x1t_ready, i + 1)
                    for t in range(T):
                        mm(mx_ps[:, t, :], x1_t[:, t, :], w1c_sb[:, :], start=True, stop=True)
                    for t in range(T):
                        last = mm(xb_ps[:, t:t + 1], x1_t[:, t, :], wb[:, :], start=True, stop=True)
                    last.then_inc(mx_done, 1)

            def step(i, odd, first=False):
                for b in range(NB):
                    if first and b + 2 < NB:
                        messages(b + 2)
                    layer0(i, b, odd, first)
                    if not first:
                        lift(i - 1, b)

            pe.wait_ge(small_loaded, 48)
            messages(0)
            messages(1)
            pe.wait_ge(wb_ready, 1)
            step(0, 0, first=True)
            with pe.Fori(1, NB - 1, 2) as i:
                step(i, 1)
                step(i + 1, 0)
            step(NB - 1, 1)

            def layer1(i, b, odd, first=False):
                n2 = NB // NA
                pe.wait_ge(adj_loaded[b % NA], (i * n2 + (b // NA + 1 + n2 * NB)) * 16)
                if first:
                    pe.wait_ge(tan_ready, b + 1)
                for t in range(T):
                    last = mm(acc1[odd][:, :], tan[:, b, t, :], pair[b % NA][:, t, :],
                              start=(b == 0 and t == 0), stop=(b == NB - 1 and t == T - 1))
                last.then_inc(l1_done, 1)

            def land(i):
                pe.wait_ge(y_o_ready, i + 1)
                for t in range(T):
                    last = nc.tensor.transpose(turned[:, t, :], o_t[:, t, :], eye_sb[:, :])
                last.then_inc(y_o_turned, 1)

            for b in range(NB):
                layer1(0, b, 0, first=True)
                lift(NB - 1, b)

            def step1(i, odd):
                for b in range(NB):
                    layer1(i, b, odd)
                    if b == 1:
                        land(i - 1)

            with pe.Fori(1, NB - 1, 2) as i:
                step1(i, 1)
                step1(i + 1, 0)
            step1(NB - 1, 1)
            land(NB - 1)


def kernel(x, adj, L0_gnn_W, L0_gnn_B, L1_gnn_weight, L1_gnn_bias):
    import concourse.bacc as bacc
    from concourse.bass_utils import run_bass_kernel_spmd

    x, adj = np.asarray(x), np.asarray(adj)
    w1 = np.asarray(L1_gnn_weight)
    arrays = {
        "x": x,
        "x_cols": x.T,
        "adj": adj.reshape(NB, BLK, NB, T, P).transpose(0, 2, 4, 3, 1),
        "w0": np.asarray(L0_gnn_W),
        "b0": np.broadcast_to(np.asarray(L0_gnn_B), (P, P)),
        "w1": w1,
        "w1_cols": w1.T,
        "b1": np.broadcast_to(np.asarray(L1_gnn_bias), (P, P)),
        "eye": np.eye(P, dtype=np.float32),
    }
    arrays = {k: np.ascontiguousarray(a) for k, a in arrays.items()}
    nc = bacc.Bacc("TRN2", target_bir_lowering=False, num_devices=1)
    args = [nc.dram_tensor(f"in_{k}", a.shape, mybir.dt.from_np(a.dtype), kind="ExternalInput").ap()
            for k, a in arrays.items()]
    x1_dram = nc.dram_tensor("x1_rows", (N, P), mybir.dt.float32).ap()
    out = nc.dram_tensor("out_y", (N, P), mybir.dt.float32, kind="ExternalOutput").ap()
    gnn_kernel(nc, *args, x1_dram, out)
    r = run_bass_kernel_spmd(nc, [{f"in_{k}": a for k, a in arrays.items()}], core_ids=[0])
    return r.results[0]["out_y"]
```

```python
from contextlib import ExitStack

import concourse.bass as bass
import numpy as np
from concourse import mybir

P = 128
N = 8192
BLK = 512
NB = N // BLK
T = BLK // P
NA = 8
NX = 4

LN_EPS = 1e-5
MIN_NORM2 = 1e-30
BALL = float(np.float32(1.0 - 1e-5))
ART_MAX = float(np.float32(1.0 - 1e-7))
BALL_GAP = (1.0 - BALL) * (1.0 + BALL)
EXP_BALL = (1.0 - BALL) / (1.0 + BALL)
P_MAX = 1.0 - 2.0 ** -24
ART_BALL = float(np.arctanh(np.float64(BALL)))
TINY_R = 1e-18

EARLY = 9


def early(i):
    return min(max(i - 1, 0), EARLY)


LATE = [(r, b) for r in range(NB) for b in range(early(r), NB)]

PRE_LINKS = 8
LIFT_LINKS = 26
LAND_LINKS = 21


def gnn_kernel(nc, x_cols, adj, w0, b0, w1, w1_cols, b1, eye, center, x1_dram, out):
    f32 = mybir.dt.float32
    ALU = mybir.AluOpType
    ACT = mybir.ActivationFunctionType
    AX = mybir.AxisListType.X

    x_blocks = x_cols.rearrange("f (n t p) -> n f t p", t=T, p=P)
    x1_blocks = x1_dram.rearrange("(n t p) f -> n p t f", t=T, p=P)
    out_blocks = out.rearrange("(n t p) f -> n p t f", t=T, p=P)

    with ExitStack() as ctx:
        def sb(name, shape):
            return ctx.enter_context(nc.sbuf_tensor(name, shape, f32))

        def pb(name, shape):
            return ctx.enter_context(nc.psum_tensor(name, shape, f32))

        def sem(name):
            return ctx.enter_context(nc.semaphore(name))

        msg = sb("msg", [P, NB, T, P])
        tan = sb("tan", [P, NB, T, P])
        x_col = tan[:, :, :, :].rearrange("p n t f -> p (n t f)")
        pair = [sb(f"pair{i}", [P, T, BLK]) for i in range(NA)]
        wt = [sb(f"wt{i}", [P, T, BLK]) for i in range(NX)]
        o_t = sb("o_t", [P, T, P])
        x_in = sb("x_in", [P, T, P])
        part = sb("part", [P, NB, BLK])
        row = sb("row", [P, T, P])
        x1_t = sb("x1_t", [P, T, P])
        mx = sb("mx", [P, T, P])
        sq = sb("sq", [P, T, P])
        w0_sb, b0_sb, w1_sb, b1_sb = (mx[:, t, :] for t in range(T))
        w1c_sb = sb("w1c_sb", [P, P])
        hb = sb("hb", [P, P])
        hb_col = sb("hb_col", [P, 1])
        wb = sb("wb", [P, 1])
        eye_sb = sb("eye_sb", [P, P])
        center_sb = sb("center_sb", [P, P])
        c = sb("c", [P, 16])
        s = sb("s", [P, 32, T])

        acc0 = [pb(f"acc0_{i}", [P, BLK]) for i in range(2)]
        acc1 = [pb(f"acc1_{i}", [P, BLK]) for i in range(2)]
        turned = pb("turned", [P, T, P])
        mx_ps = pb("mx_ps", [P, T, P])
        xb_ps = pb("xb_ps", [P, T])

        small_loaded = sem("small_loaded")
        eye_loaded = sem("eye_loaded")
        xcol_loaded = [sem(f"xcol_loaded{i}") for i in range(4)]
        adj_loaded = [sem(f"adj_loaded{i}") for i in range(NA)]
        xin_loaded = sem("xin_loaded")
        x1_stored = sem("x1_stored")
        out_stored = sem("out_stored")
        bias_sq = sem("bias_sq")
        bias_exp = sem("bias_exp")
        hb_ready = sem("hb_ready")
        hb_turned = sem("hb_turned")
        hbcol_ready = sem("hbcol_ready")
        wb_done = sem("wb_done")
        wb_ready = sem("wb_ready")
        msg_done = sem("msg_done")
        msg_ready = sem("msg_ready")
        ln_ready = sem("ln_ready")
        inv_ready = sem("inv_ready")
        z_ready = sem("z_ready")
        e_ready = sem("e_ready")
        w_ready = sem("w_ready")
        l0_done = sem("l0_done")
        late_done = sem("late_done")
        row_done = sem("row_done")
        act_ln = sem("act_ln")
        dve_step = sem("dve_step")
        act_step = sem("act_step")
        o_ready = sem("o_ready")
        o_turned = sem("o_turned")
        var_ready = sem("var_ready")
        rstd_ready = sem("rstd_ready")
        x1_ready = sem("x1_ready")
        x1_turned = sem("x1_turned")
        x1t_ready = sem("x1t_ready")
        mx_done = sem("mx_done")
        norms_ready = sem("norms_ready")
        roots_ready = sem("roots_ready")
        clip_ready = sem("clip_ready")
        art_ready = sem("art_ready")
        arg_ready = sem("arg_ready")
        tanh_ready = sem("tanh_ready")
        sum_ready = sem("sum_ready")
        sumroot_ready = sem("sumroot_ready")
        sumclip_ready = sem("sumclip_ready")
        sumart_ready = sem("sumart_ready")
        tan_ready = sem("tan_ready")
        y_o_ready = sem("y_o_ready")
        y_o_turned = sem("y_o_turned")
        y_norms_ready = sem("y_norms_ready")
        y_roots_ready = sem("y_roots_ready")
        y_arg_ready = sem("y_arg_ready")
        y_tanh_ready = sem("y_tanh_ready")
        y_var_ready = sem("y_var_ready")
        y_rstd_ready = sem("y_rstd_ready")
        y_ready = sem("y_ready")
        y_xin_loaded = sem("y_xin_loaded")

        block = ctx.enter_context(nc.Block())

        def q(k, n=1):
            return s[:, k:k + n, :]

        def wide(k):
            return s[:, k, :].unsqueeze(2).to_broadcast([P, T, P])

        def late_count(m):
            r = LATE[m][0]
            if m + 1 == len(LATE) or LATE[m + 1][0] != r:
                return row_done, r + 1
            return late_done, m + 1 - r

        @block.sync
        def _(sp):
            def load(i, b):
                k = b % NA
                sp.dma_start(pair[k][:, :, :], adj[i, b]).then_inc(adj_loaded[k], 16)

            for dst, src in ((w0_sb, w0), (b0_sb, b0), (b1_sb, b1)):
                sp.dma_start(dst, src).then_inc(small_loaded, 16)
            for i in range(4):
                cols = slice(i * N // 4, (i + 1) * N // 4)
                sp.dma_start(x_col[:, cols], x_cols[:, cols]).then_inc(xcol_loaded[i], 16)
                if i < 2:
                    load(0, i)
            for dst, src in ((w1_sb, w1), (w1c_sb[:, :], w1_cols), (eye_sb[:, :], eye), (center_sb[:, :], center)):
                sp.dma_start(dst, src).then_inc(eye_loaded, 16)
            def freed(n):
                sp.wait_ge(l0_done, n - NA + 2)

            for b in range(2, NB):
                if b >= NA:
                    freed(b)
                load(0, b)
            with sp.Fori(1, NB) as i:
                for b in range(NB):
                    freed(i * NB + b)
                    load(i, b)
            for m, (r, b) in enumerate(LATE):
                if m < NA:
                    sp.wait_ge(l0_done, min(NB * NB + m - NA + 2, NB * NB))
                else:
                    sem_, value = late_count(m - NA)
                    sp.wait_ge(sem_, value)
                sp.dma_start(pair[m % NA][:, :, :], adj[r, b]).then_inc(adj_loaded[m % NA], 16)

        @block.gpsimd
        def _(pool):
            pool.dma_start(x_in[:, :, :], x_blocks[0]).then_inc(xin_loaded, 16)

            def store_x1(i):
                pool.wait_ge(x1_ready, i + 1)
                pool.dma_start(x1_blocks[i], row[:, :, :]).then_inc(x1_stored, 16)
                pool.wait_ge(x1_stored, (i + 1) * 16)

            with pool.Fori(0, NB - 1) as i:
                store_x1(i)
                pool.dma_start(x_in[:, :, :], x_blocks[i + 1]).then_inc(xin_loaded, 16)
            store_x1(NB - 1)
            pool.dma_start(x_in[:, :, :], x1_blocks[0]).then_inc(y_xin_loaded, 16)

            def store_y(i):
                pool.wait_ge(y_ready, i + 1)
                pool.dma_start(out_blocks[i], row[:, :, :]).then_inc(out_stored, 16)
                pool.wait_ge(out_stored, (i + 1) * 16)

            with pool.Fori(0, NB - 1) as i:
                store_y(i)
                pool.dma_start(x_in[:, :, :], x1_blocks[i + 1]).then_inc(y_xin_loaded, 16)
            store_y(NB - 1)

        @block.scalar
        def _(act):
            nc.scalar.preload_act_table_set("natural_log_exp_and_others")

            def chained(ins, count):
                ins.then_inc(act_step, 1)
                act.wait_ge(act_step, count)

            act.wait_ge(bias_sq, 1)
            chained(nc.scalar.activation(c[:, 1:2], c[:, 0:1], ACT.Ln), 1)
            nc.scalar.activation(c[:, 2:3], c[:, 1:2], ACT.Exp, scale=-0.5)
            chained(nc.scalar.activation(c[:, 3:4], c[:, 1:2], ACT.Exp, scale=0.5), 2)
            nc.scalar.activation(c[:, 4:5], c[:, 3:4], ACT.Exp, scale=-2.0).then_inc(bias_exp, 1)

            def logs(i, b):
                k = b % NA
                act.wait_ge(adj_loaded[k], (i * (NB // NA) + (b // NA + 1)) * 16)
                if not (isinstance(i, int) and i * NB + b < NX):
                    act.wait_ge(l0_done, i * NB + (b - NX + 1))
                nc.scalar.activation(wt[b % NX][:, :, :], pair[k][:, :, :], ACT.Ln,
                                     bias=TINY_R).then_inc(ln_ready, 1)

            def inverses(i, b):
                act.wait_ge(ln_ready, i * NB + (b + 1))
                nc.scalar.activation(wt[b % NX][:, :, :], wt[b % NX][:, :, :], ACT.Exp,
                                     scale=-2.0).then_inc(inv_ready, 1)

            def exps(i, b):
                act.wait_ge(z_ready, i * NB + (b + 1))
                nc.scalar.activation(wt[b % NX][:, :, :], wt[b % NX][:, :, :], ACT.Exp,
                                     bias=-2.0, scale=4.0).then_inc(e_ready, 1)

            def lift(i, b):
                if b == 3:
                    act.wait_ge(var_ready, i + 1)
                    chained(nc.scalar.activation(q(1), q(0), ACT.Ln, scale=1.0 / P, bias=LN_EPS), i * 2 + 3)
                    nc.scalar.activation(q(2), q(1), ACT.Exp, scale=-0.5).then_inc(rstd_ready, 1)
                if b == 9:
                    act.wait_ge(norms_ready, i + 1)
                    chained(nc.scalar.activation(q(6, 2), q(4, 2), ACT.Ln), i * 2 + 4)
                    nc.scalar.activation(q(8), q(6), ACT.Exp, scale=0.5)
                    nc.scalar.activation(q(9), q(7), ACT.Exp, scale=-0.5).then_inc(roots_ready, 1)
                if b == 10:
                    act.wait_ge(clip_ready, i + 1)
                    nc.scalar.activation(q(12), q(10), ACT.Ln, bias=1.0)
                    nc.scalar.activation(q(13), q(10), ACT.Ln, scale=-1.0, bias=1.0)
                    nc.scalar.activation(q(14), q(11), ACT.Exp, scale=0.5).then_inc(art_ready, 1)
                if b == 11:
                    act.wait_ge(arg_ready, i + 1)
                    nc.scalar.activation(q(16), q(15), ACT.Exp, scale=-1.0).then_inc(tanh_ready, 1)
                if b == 13:
                    act.wait_ge(sum_ready, i + 1)
                    nc.scalar.activation(q(24), q(23), ACT.Ln, scale=-1.0, bias=1.0).then_inc(act_ln, 1)
                    act.wait_ge(act_ln, i + 1)
                    nc.scalar.activation(q(25), q(24), ACT.Exp, scale=0.5)
                    nc.scalar.activation(q(26), q(24), ACT.Exp, scale=-0.5)
                    nc.scalar.activation(q(29), q(22), ACT.Ln).then_inc(sumroot_ready, 1)
                if b == 14:
                    act.wait_ge(sumclip_ready, i + 1)
                    nc.scalar.activation(q(28), q(27), ACT.Ln, bias=1.0).then_inc(sumart_ready, 1)

            def step(i, first=False, last=False):
                for b in range(NB):
                    ahead = not (last and b + 2 >= NB)
                    if ahead:
                        logs(i, b + 2)
                    exps(i, b)
                    if ahead:
                        inverses(i, b + 2)
                    if not first:
                        lift(i - 1, b)

            for b in range(2):
                logs(0, b)
                inverses(0, b)
            step(0, first=True)
            with act.Fori(1, NB - 1) as i:
                step(i)
            step(NB - 1, last=True)
            for b in range(NB):
                lift(NB - 1, b)

            def land(i):
                act.wait_ge(y_norms_ready, i + 1)
                chained(nc.scalar.activation(q(6, 2), q(4, 2), ACT.Ln), i * 2 + 3 + 2 * NB)
                nc.scalar.activation(q(8), q(6), ACT.Exp, scale=0.5)
                nc.scalar.activation(q(9), q(6), ACT.Exp, scale=-0.5)
                nc.scalar.activation(q(10), q(7), ACT.Exp, scale=0.5)
                nc.scalar.activation(q(11), q(7), ACT.Exp, scale=-0.5).then_inc(y_roots_ready, 1)
                act.wait_ge(y_arg_ready, i + 1)
                nc.scalar.activation(q(13), q(12), ACT.Exp, scale=-2.0).then_inc(y_tanh_ready, 1)
                act.wait_ge(y_var_ready, i + 1)
                chained(nc.scalar.activation(q(1), q(0), ACT.Ln, scale=1.0 / P, bias=LN_EPS),
                        i * 2 + 4 + 2 * NB)
                nc.scalar.activation(q(2), q(1), ACT.Exp, scale=-0.5).then_inc(y_rstd_ready, 1)

            with act.Fori(0, NB) as i:
                land(i)

        @block.vector
        def _(dve):
            v = nc.vector
            state = {"base": 0, "count": 0}

            def mark(ins):
                state["count"] += 1
                ins.then_inc(dve_step, 1)

            def after_mark():
                dve.wait_ge(dve_step, state["base"] + state["count"])

            def link(ins):
                mark(ins)
                after_mark()

            def links(base, count, body):
                state["base"], state["count"] = base, 0
                body()
                assert state["count"] == count, state["count"]

            def pre():
                v.memset(part[:, 0:2, :], 0.0)
                dve.wait_ge(small_loaded, 48)
                link(v.tensor_tensor(hb[:, :], b1_sb, b1_sb, ALU.mult))
                link(v.tensor_reduce(c[:, 5:6], hb[:, :], AX, ALU.add))
                v.tensor_scalar(c[:, 0:1], c[:, 5:6], MIN_NORM2, None, ALU.max).then_inc(bias_sq, 1)
                dve.wait_ge(bias_exp, 1)
                v.tensor_scalar(c[:, 6:7], c[:, 4:5], -1.0, 1.0, ALU.mult, ALU.add)
                link(v.tensor_scalar(c[:, 7:8], c[:, 4:5], 1.0, None, ALU.add))
                link(v.reciprocal(c[:, 8:9], c[:, 7:8]))
                link(v.tensor_scalar(c[:, 9:10], c[:, 6:7], c[:, 8:9], BALL, ALU.mult, ALU.min))
                v.tensor_scalar(hb[:, :], b1_sb, c[:, 9:10], c[:, 2:3], ALU.mult, ALU.mult).then_inc(hb_ready, 1)
                v.tensor_scalar(c[:, 5:6], c[:, 9:10], -1.0, 1.0, ALU.mult, ALU.add)
                link(v.tensor_tensor(c[:, 10:11], c[:, 9:10], c[:, 9:10], ALU.mult))
                v.tensor_scalar(c[:, 11:12], c[:, 10:11], 1.0, None, ALU.add)
                v.tensor_scalar(c[:, 12:13], c[:, 10:11], -1.0, None, ALU.mult)
                link(v.tensor_scalar(c[:, 6:7], c[:, 9:10], 1.0, None, ALU.add))
                link(v.tensor_tensor(c[:, 3:4], c[:, 5:6], c[:, 6:7], ALU.mult))
                dve.wait_ge(hb_turned, 1)
                v.tensor_copy(hb_col[:, :], turned[:, 0, 0:1]).then_inc(hbcol_ready, 1)
                dve.wait_ge(wb_done, 1)
                v.tensor_copy(wb[:, :], xb_ps[:, 0:1]).then_inc(wb_ready, 1)

            links(0, PRE_LINKS, pre)

            def messages(b):
                dve.wait_ge(msg_done, b + 1)
                v.tensor_tensor(msg[:, b, :, :], acc1[b % 2][:, :].rearrange("p (t f) -> p t f", t=T),
                                b0_sb.unsqueeze(1).to_broadcast([P, T, P]), ALU.add).then_inc(msg_ready, 1)

            def halves(i, b):
                buf = wt[b % NX][:, :, :]
                dve.wait_ge(inv_ready, i * NB + (b + 1))
                v.scalar_tensor_tensor(buf, pair[b % NA][:, :, :], 0.5, buf, ALU.subtract, ALU.mult).then_inc(z_ready, 1)

            def masks(i, b):
                buf = wt[b % NX][:, :, :]
                dve.wait_ge(e_ready, i * NB + (b + 1))
                v.scalar_tensor_tensor(buf, pair[b % NA][:, :, :], 1.0, buf, ALU.is_lt, ALU.mult).then_inc(w_ready, 1)

            def deviations():
                link(v.tensor_reduce(q(3), row[:, :, :], AX, ALU.add))
                link(v.tensor_scalar(q(1), q(3), -1.0 / P, None, ALU.mult))
                link(v.tensor_tensor(row[:, :, :], row[:, :, :], wide(1), ALU.add))
                link(v.tensor_tensor(sq[:, :, :], row[:, :, :], row[:, :, :], ALU.mult))
                return v.tensor_reduce(q(0), sq[:, :, :], AX, ALU.add)

            def refined_rstd():
                v.tensor_scalar(q(30), q(0), 1.0 / P, LN_EPS, ALU.mult, ALU.add)
                link(v.scalar_tensor_tensor(q(31), q(2), -0.5, q(2), ALU.mult, ALU.mult))
                link(v.tensor_tensor(q(30), q(30), q(31), ALU.mult))
                link(v.scalar_tensor_tensor(q(3), q(30), 1.5, q(2), ALU.add, ALU.mult))

            def lift(i, k, early_sums=True):
                if k == 1:
                    dve.wait_ge(l0_done, (i + 1) * NB)
                    if early_sums:
                        v.tensor_copy(part[:, i, :], acc1[lift_marks["acc"]][:, :])
                    v.tensor_copy(o_t[:, :, :].rearrange("p t f -> p (t f)"),
                                  acc0[lift_marks["acc"]][:, :]).then_inc(o_ready, 1)
                if k == 4:
                    dve.wait_ge(o_turned, i + 1)
                    mark(v.tensor_copy(row[:, :, :], turned[:, :, :]))
                if k == 5:
                    after_mark()
                    mark(v.tensor_tensor(sq[:, :, :], row[:, :, :], row[:, :, :], ALU.mult))
                if k == 6:
                    after_mark()
                    v.tensor_reduce(q(0), sq[:, :, :], AX, ALU.add).then_inc(var_ready, 1)
                if k == 8:
                    dve.wait_ge(rstd_ready, i + 1)
                    v.tensor_scalar(q(30), q(0), 1.0 / P, LN_EPS, ALU.mult, ALU.add)
                    mark(v.scalar_tensor_tensor(q(31), q(2), -0.5, q(2), ALU.mult, ALU.mult))
                if k == 9:
                    after_mark()
                    link(v.tensor_tensor(q(30), q(30), q(31), ALU.mult))
                    mark(v.scalar_tensor_tensor(q(3), q(30), 1.5, q(2), ALU.add, ALU.mult))
                if k == 10:
                    after_mark()
                    v.tensor_tensor(row[:, :, :], row[:, :, :], wide(3), ALU.mult).then_inc(x1_ready, 1)
                    mark(v.tensor_tensor(q(30), q(0), q(3), ALU.mult))
                if k == 11:
                    after_mark()
                    link(v.tensor_tensor(q(31), q(30), q(3), ALU.mult))
                    v.tensor_scalar(q(4), q(31), MIN_NORM2, None, ALU.max)
                if k == 13:
                    dve.wait_ge(x1_turned, i + 1)
                    v.tensor_copy(x1_t[:, :, :], turned[:, :, :]).then_inc(x1t_ready, 1)
                if k == 15:
                    dve.wait_ge(mx_done, i + 1)
                    v.tensor_copy(q(17), xb_ps[:, :].unsqueeze(1))
                    mark(v.tensor_copy(mx[:, :, :], mx_ps[:, :, :]))
                if k == 16:
                    after_mark()
                    mark(v.tensor_tensor(sq[:, :, :], mx[:, :, :], mx[:, :, :], ALU.mult))
                if k == 17:
                    after_mark()
                    mark(v.tensor_reduce(q(31), sq[:, :, :], AX, ALU.add))
                if k == 18:
                    after_mark()
                    v.tensor_scalar(q(5), q(31), MIN_NORM2, None, ALU.max).then_inc(norms_ready, 1)
                if k == 20:
                    dve.wait_ge(roots_ready, i + 1)
                    v.tensor_scalar(q(10), q(8), ART_MAX, None, ALU.min)
                    v.tensor_tensor(q(11), q(7), q(6), ALU.subtract).then_inc(clip_ready, 1)
                if k == 22:
                    dve.wait_ge(art_ready, i + 1)
                    link(v.tensor_tensor(q(15), q(12), q(13), ALU.subtract))
                    v.tensor_tensor(q(15), q(15), q(14), ALU.mult).then_inc(arg_ready, 1)
                if k == 24:
                    dve.wait_ge(tanh_ready, i + 1)
                    v.tensor_scalar(q(18), q(16), EXP_BALL, None, ALU.max)
                    link(v.tensor_scalar(q(19), q(16), EXP_BALL, 1.0, ALU.max, ALU.add))
                    link(v.reciprocal(q(20), q(19)))
                    v.tensor_scalar(q(19), q(20), 2.0, -1.0, ALU.mult, ALU.add)
                    mark(v.tensor_tensor(q(21), q(18), q(20), ALU.mult))
                if k == 25:
                    after_mark()
                    v.scalar_tensor_tensor(q(18), q(21), 4.0, q(20), ALU.mult, ALU.mult)
                    link(v.tensor_tensor(q(19), q(19), q(9), ALU.mult))
                    link(v.tensor_tensor(q(17), q(17), q(19), ALU.mult))
                    link(v.tensor_scalar(q(21), q(17), 2.0, c[:, 11:12], ALU.mult, ALU.add))
                    mark(v.scalar_tensor_tensor(q(31), q(18), c[:, 12:13], q(21), ALU.mult, ALU.add))
                if k == 26:
                    after_mark()
                    v.tensor_tensor(q(21), q(21), q(19), ALU.mult)
                    link(v.tensor_scalar(q(31), q(31), 1e-15, None, ALU.max))
                    link(v.reciprocal(q(30), q(31)))
                    link(v.scalar_tensor_tensor(q(31), q(18), c[:, 3:4], q(30), ALU.mult, ALU.mult))
                    v.tensor_scalar(q(22), q(31), BALL_GAP, P_MAX, ALU.max, ALU.min)
                    v.tensor_scalar(q(23), q(31), P_MAX, None, ALU.min).then_inc(sum_ready, 1)
                if k == 28:
                    dve.wait_ge(sumroot_ready, i + 1)
                    v.tensor_scalar(q(27), q(25), BALL, None, ALU.min).then_inc(sumclip_ready, 1)
                    mark(v.tensor_tensor(q(24), q(26), q(30), ALU.mult))
                if k == 30:
                    dve.wait_ge(sumart_ready, i + 1)
                    after_mark()
                    link(v.scalar_tensor_tensor(q(31), q(29), -0.5, q(28), ALU.mult, ALU.add))
                    link(v.tensor_tensor(q(31), q(31), q(24), ALU.mult))
                    v.tensor_tensor(q(23), q(18), q(31), ALU.mult)
                    mark(v.tensor_tensor(q(22), q(21), q(31), ALU.mult))
                if k == 31:
                    after_mark()
                    hb_wide = hb[:, :].unsqueeze(1).to_broadcast([P, T, P])
                    v.tensor_tensor(mx[:, :, :], mx[:, :, :], wide(22), ALU.mult)
                    link(v.tensor_tensor(sq[:, :, :], hb_wide, wide(23), ALU.mult))
                    v.tensor_tensor(tan[:, i, :, :], mx[:, :, :], sq[:, :, :], ALU.add).then_inc(tan_ready, 1)

            lift_marks = {"acc": None}

            def step(i, odd, first=False, last=False, early_sums=True):
                lift_marks["acc"] = 1 - odd

                def body():
                    for b in range(NB):
                        if first:
                            messages(b)
                        if not (last and b + 1 >= NB):
                            halves(i, b + 1)
                        if not first:
                            lift(i - 1, 2 * b, early_sums)
                        masks(i, b)
                        if not first:
                            lift(i - 1, 2 * b + 1, early_sums)

                links(PRE_LINKS + (i - 1) * LIFT_LINKS, 0 if first else LIFT_LINKS, body)

            halves(0, 0)
            step(0, 0, first=True)
            step(1, 1, early_sums=False)
            step(2, 0, early_sums=False)
            with dve.Fori(3, NB - 1, 2) as i:
                step(i, 1)
                step(i + 1, 0)
            step(NB - 1, 1, last=True)
            lift_marks["acc"] = 1
            links(PRE_LINKS + (NB - 1) * LIFT_LINKS, LIFT_LINKS,
                  lambda: [lift(NB - 1, k) for k in range(2 * NB)])

            def land(i, odd):
                dve.wait_ge(row_done, i + 1)
                v.tensor_tensor(o_t[:, :, :].rearrange("p t f -> p (t f)"), acc1[odd][:, :], part[:, i, :],
                                ALU.add).then_inc(y_o_ready, 1)
                dve.wait_ge(y_o_turned, i + 1)
                link(v.tensor_copy(mx[:, :, :], turned[:, :, :]))
                v.tensor_scalar(x1_t[:, :, :], mx[:, :, :], 0.0, None, ALU.max)
                link(v.tensor_tensor(sq[:, :, :], mx[:, :, :], mx[:, :, :], ALU.mult))
                link(v.tensor_reduce(q(30), sq[:, :, :], AX, ALU.add))
                link(v.tensor_tensor(sq[:, :, :], x1_t[:, :, :], x1_t[:, :, :], ALU.mult))
                link(v.tensor_reduce(q(31), sq[:, :, :], AX, ALU.add))
                v.tensor_scalar(q(4, 2), q(30, 2), MIN_NORM2, None, ALU.max).then_inc(y_norms_ready, 1)
                dve.wait_ge(y_roots_ready, i + 1)
                link(v.tensor_scalar(q(12), q(8), ART_BALL, None, ALU.min))
                link(v.tensor_tensor(q(14), q(12), q(9), ALU.mult))
                v.tensor_tensor(q(12), q(14), q(10), ALU.mult).then_inc(y_arg_ready, 1)
                dve.wait_ge(y_tanh_ready, i + 1)
                v.tensor_scalar(q(15), q(13), -1.0, 1.0, ALU.mult, ALU.add)
                link(v.tensor_scalar(q(16), q(13), 1.0, None, ALU.add))
                link(v.reciprocal(q(17), q(16)))
                link(v.tensor_tensor(q(15), q(15), q(17), ALU.mult))
                link(v.tensor_scalar(q(15), q(15), BALL, None, ALU.min))
                link(v.tensor_tensor(q(18), q(15), q(11), ALU.mult))
                link(v.tensor_tensor(x1_t[:, :, :], x1_t[:, :, :], wide(18), ALU.mult))
                dve.wait_ge(y_xin_loaded, (i + 1) * 16)
                link(v.tensor_tensor(row[:, :, :], x1_t[:, :, :], x_in[:, :, :], ALU.add))
                deviations().then_inc(y_var_ready, 1)
                dve.wait_ge(y_rstd_ready, i + 1)
                refined_rstd()
                v.tensor_tensor(row[:, :, :], row[:, :, :], wide(3), ALU.mult).then_inc(y_ready, 1)

            def land_step(i, odd):
                links(PRE_LINKS + NB * LIFT_LINKS + i * LAND_LINKS, LAND_LINKS, lambda: land(i, odd))

            land_step(0, 0)
            with dve.Fori(1, NB - 1, 2) as i:
                land_step(i, 1)
                land_step(i + 1, 0)
            land_step(NB - 1, 1)

        @block.tensor
        def _(pe):
            mm = nc.tensor.matmul

            pe.wait_ge(eye_loaded, 64)
            pe.wait_ge(hb_ready, 1)
            nc.tensor.transpose(turned[:, 0, :], hb[:, :], eye_sb[:, :]).then_inc(hb_turned, 1)
            pe.wait_ge(hbcol_ready, 1)
            mm(xb_ps[:, 0:1], w1_sb, hb_col[:, :], start=True, stop=True).then_inc(wb_done, 1)

            def messages(b):
                if b % 4 == 0:
                    pe.wait_ge(xcol_loaded[b // 4], 16)
                if b >= 2:
                    pe.wait_ge(msg_ready, b - 1)
                for t in range(T):
                    col = (b * T + t) * P
                    last = mm(acc1[b % 2][:, t * P:(t + 1) * P], x_col[:, col:col + P], w0_sb,
                              start=True, stop=True)
                last.then_inc(msg_done, 1)

            def layer0(i, b, odd, first):
                if first:
                    pe.wait_ge(msg_ready, b + 1)
                pe.wait_ge(w_ready, i * NB + (b + 1))
                for t in range(T):
                    last = mm(acc0[odd][:, :], msg[:, b, t, :], wt[b % NX][:, t, :],
                              start=(b == 0 and t == 0), stop=(b == NB - 1 and t == T - 1))
                last.then_inc(l0_done, 1)

            def lift(i, b):
                if b == 0:
                    pe.wait_ge(o_ready, i + 1)
                    pe.wait_ge(xin_loaded, (i + 1) * 16)
                    for t in range(T):
                        mm(turned[:, t, :], o_t[:, t, :], center_sb[:, :], start=True, stop=False)
                        last = mm(turned[:, t, :], x_in[:, t, :], center_sb[:, :], start=False, stop=True)
                    last.then_inc(o_turned, 1)
                if b == 5:
                    pe.wait_ge(x1_ready, i + 1)
                    for t in range(T):
                        last = nc.tensor.transpose(turned[:, t, :], row[:, t, :], eye_sb[:, :])
                    last.then_inc(x1_turned, 1)
                if b == 6:
                    pe.wait_ge(x1t_ready, i + 1)
                    for t in range(T):
                        mm(mx_ps[:, t, :], x1_t[:, t, :], w1c_sb[:, :], start=True, stop=True)
                    for t in range(T):
                        last = mm(xb_ps[:, t:t + 1], x1_t[:, t, :], wb[:, :], start=True, stop=True)
                    last.then_inc(mx_done, 1)

            def early_layer1(b, odd):
                for t in range(T):
                    mm(acc1[odd][:, :], tan[:, b, t, :], pair[b % NA][:, t, :],
                       start=(b == 0 and t == 0), stop=(t == T - 1), skip_group_check=True)

            def step(i, odd, first=False):
                if not first and not (isinstance(i, int) and i == 1):
                    pe.wait_ge(tan_ready, i - 1)
                for b in range(NB):
                    if first and b + 2 < NB:
                        messages(b + 2)
                    layer0(i, b, odd, first)
                    if not first:
                        lift(i - 1, b)
                    if isinstance(i, int):
                        if b < early(i):
                            early_layer1(b, odd)
                    elif b < early(3):
                        early_layer1(b, odd)
                    elif b < EARLY:
                        with pe.If(i >= b + 2):
                            early_layer1(b, odd)

            pe.wait_ge(small_loaded, 48)
            messages(0)
            messages(1)
            pe.wait_ge(wb_ready, 1)
            step(0, 0, first=True)
            step(1, 1)
            step(2, 0)
            with pe.Fori(3, NB - 1, 2) as i:
                step(i, 1)
                step(i + 1, 0)
            step(NB - 1, 1)

            def late_layer1(m):
                r, b = LATE[m]
                pe.wait_ge(adj_loaded[m % NA], (NB * NB // NA + m // NA + 1) * 16)
                if r == 0:
                    pe.wait_ge(tan_ready, b + 1)
                for t in range(T):
                    last = mm(acc1[r % 2][:, :], tan[:, b, t, :], pair[m % NA][:, t, :],
                              start=(b == early(r) and t == 0), stop=(b == NB - 1 and t == T - 1))
                last.then_inc(late_count(m)[0], 1)

            def land(i):
                pe.wait_ge(y_o_ready, i + 1)
                for t in range(T):
                    last = nc.tensor.transpose(turned[:, t, :], o_t[:, t, :], eye_sb[:, :])
                last.then_inc(y_o_turned, 1)

            for m, (r, b) in enumerate(LATE):
                late_layer1(m)
                if r == 0:
                    lift(NB - 1, b)
                elif b == early(r) + 1:
                    land(r - 1)
            land(NB - 1)


def kernel(x, adj, L0_gnn_W, L0_gnn_B, L1_gnn_weight, L1_gnn_bias):
    import concourse.bacc as bacc
    from concourse.bass_utils import run_bass_kernel_spmd

    x, adj = np.asarray(x), np.asarray(adj)
    w1 = np.asarray(L1_gnn_weight)
    arrays = {
        "x_cols": x.T,
        "adj": adj.reshape(NB, BLK, NB, T, P).transpose(0, 2, 4, 3, 1),
        "w0": np.asarray(L0_gnn_W),
        "b0": np.broadcast_to(np.asarray(L0_gnn_B), (P, P)),
        "w1": w1,
        "w1_cols": w1.T,
        "b1": np.broadcast_to(np.asarray(L1_gnn_bias), (P, P)),
        "eye": np.eye(P, dtype=np.float32),
        "center": np.eye(P, dtype=np.float32) - np.float32(1.0 / P),
    }
    arrays = {k: np.ascontiguousarray(a) for k, a in arrays.items()}
    nc = bacc.Bacc("TRN2", target_bir_lowering=False, num_devices=1)
    args = [nc.dram_tensor(f"in_{k}", a.shape, mybir.dt.from_np(a.dtype), kind="ExternalInput").ap()
            for k, a in arrays.items()]
    x1_dram = nc.dram_tensor("x1_rows", (N, P), mybir.dt.float32).ap()
    out = nc.dram_tensor("out_y", (N, P), mybir.dt.float32, kind="ExternalOutput").ap()
    gnn_kernel(nc, *args, x1_dram, out)
    r = run_bass_kernel_spmd(nc, [{f"in_{k}": a for k, a in arrays.items()}], core_ids=[0])
    return r.results[0]["out_y"]
```

```python
from contextlib import ExitStack

import concourse.bass as bass
import numpy as np
from concourse import mybir

P = 128
N = 8192
BLK = 512
NB = N // BLK
T = BLK // P
NA = 8
NX = 4

LN_EPS = 1e-5
MIN_NORM2 = 1e-30
BALL = float(np.float32(1.0 - 1e-5))
ART_MAX = float(np.float32(1.0 - 1e-7))
BALL_GAP = (1.0 - BALL) * (1.0 + BALL)
EXP_BALL = (1.0 - BALL) / (1.0 + BALL)
P_MAX = 1.0 - 2.0 ** -24
ART_BALL = float(np.arctanh(np.float64(BALL)))
TINY_R = 1e-18


PLACE, MX_SLACK, W_SLACK = 5.68, 0.0, 7.0
EXTRA_ROW = {4: NB - 1, 5: NB - 2, 6: NB - 1}


def early_jobs():
    place, product = PLACE, 3.43
    lift = {0: 0.9, 5: 0.5, 6: 0.9}

    def in_time(start, b):
        for k in range(b, b + 4):
            ready = k * place
            if k % NB == 6:
                start = max(start, ready + 0.7) + lift[6]
                if start > ready + place + MX_SLACK:
                    return False
            start = max(start, ready) + product + (lift[k % NB] if k % NB in (0, 5) else 0.0)
            if start > ready + W_SLACK:
                return False
        return True

    own, other, extra = ([[] for _ in range(NB)] for _ in range(3))
    ahead = {r: set() for r in range(NB)}
    now = 0.0
    for i in range(NB):
        row = i - 3
        open_ = [b for b in range(i - 1) if b not in own[row]] if row >= 0 else []
        for b in range(NB):
            now = max(now, b * place) + product + lift.get(b, 0.0)
            if b == NB - 1 or not in_time(now + product, b + 1):
                continue
            if b <= i - 2 and b not in ahead[i]:
                own[i].append(b)
            elif open_:
                other[i].append((b, open_.pop()))
            elif i in EXTRA_ROW and 2 <= b < NB - 2 and set(range(i - 1)) - ahead[EXTRA_ROW[i]]:
                column = min(set(range(i - 1)) - ahead[EXTRA_ROW[i]])
                ahead[EXTRA_ROW[i]].add(column)
                extra[i].append((b, column))
            else:
                continue
            now += product
        now -= NB * place
    return own, other, extra


OWN, OTHER, EXTRA = early_jobs()
EARLY = {(i, b) for i in range(NB) for b in OWN[i]} | {(i - 3, b) for i in range(3, NB) for _, b in OTHER[i]}
EARLY |= {(r, b) for i, r in EXTRA_ROW.items() for _, b in EXTRA[i]}
LATE = [(r, b) for r in range(NB) for b in range(NB) if (r, b) not in EARLY]


assert all(OWN[2:]) and not any(OWN[:2]) and all(OTHER[3:NB - 1]) and not any(OTHER[:3])


def late_row(r):
    return [b for q, b in LATE if q == r]


NL = 7
NO = 3
OTHERS = sorted([(i, at, i - 3, b) for i in range(NB) for at, b in OTHER[i]]
                + [(i, at, r, b) for i, r in EXTRA_ROW.items() for at, b in EXTRA[i]])
assert all(EXTRA[i] for i in EXTRA_ROW)

NS = 2
HALVES = (slice(0, T // 2), slice(T // 2, T))
WHOLE = (1, 4, 7)
SPLIT = [m for m, (r, b) in enumerate(LATE) if r > 0 and late_row(r).index(b) not in WHOLE]
ROW_ENDS = [max(m for m, (q, _) in enumerate(LATE) if q == r) for r in range(NB)]
LAND_VECTOR = (3, 9, 10, 12, 14, 15, 16, 17, 18, 20, 22, 23)
LAND_SCALAR = (8, 11, 13, 19, 21)
LAND_APART = 14
LAND_FROM = [2 * ROW_ENDS[0]]
for r in range(1, NB):
    LAND_FROM.append(max(2 * ROW_ENDS[r], LAND_FROM[-1] + LAND_APART))
assert LAND_SCALAR[0] + LAND_APART > LAND_SCALAR[3] and LAND_VECTOR[1] + LAND_APART >= LAND_VECTOR[-1]
LAND_TENSOR = 4
assert all(LAND_FROM[r] + LAND_TENSOR <= 2 * ROW_ENDS[r + 1] for r in range(NB - 1))
SLOTS = LAND_FROM[-1] + max(LAND_VECTOR)

PRE_LINKS = 8
LIFT_LINKS = 26


def gnn_kernel(nc, x_cols, adj, w0, b0, w1, w1_cols, b1, eye, center, x1_dram, part_dram, out):
    f32 = mybir.dt.float32
    ALU = mybir.AluOpType
    ACT = mybir.ActivationFunctionType
    AX = mybir.AxisListType.X

    x_blocks = x_cols.rearrange("f (n t p) -> n f t p", t=T, p=P)
    x1_blocks = x1_dram.rearrange("(n t p) f -> n p t f", t=T, p=P)
    out_blocks = out.rearrange("(n t p) f -> n p t f", t=T, p=P)

    with ExitStack() as ctx:
        f32r = mybir.dt.float32r

        def sb(name, shape, dtype=f32, stack=ctx):
            return stack.enter_context(nc.sbuf_tensor(name, shape, dtype))

        def pb(name, shape):
            return ctx.enter_context(nc.psum_tensor(name, shape, f32))

        def sem(name):
            return ctx.enter_context(nc.semaphore(name))

        tan = sb("tan", [P, NB, T, P])
        x_col = tan[:, :, :, :].rearrange("p n t f -> p (n t f)")
        pair = [sb(f"pair{i}", [P, T, BLK]) for i in range(NL)]
        o_t = sb("o_t", [P, T, P])
        x_in = sb("x_in", [P, T, P])
        part = sb("part", [P, 2, BLK])
        extra = sb("extra", [P, 2, BLK])
        row = sb("row", [P, T, P])
        x1_t = sb("x1_t", [P, T, P])
        mx = sb("mx", [P, T, P])
        sq = sb("sq", [P, T, P])
        w0_sb, b0_sb, w1_sb, b1_sb = (mx[:, t, :] for t in range(T))
        w1c_sb = sb("w1c_sb", [P, P + 1])
        hb = sb("hb", [P, P])
        hb_col = sb("hb_col", [P, 1])
        eye_sb = sb("eye_sb", [P, P])
        center_sb = sb("center_sb", [P, P])
        c = sb("c", [P, 16])
        s = sb("s", [P, 32, T])

        with ExitStack() as first:
            pair += [sb(f"pair{i}", [P, T, BLK], stack=first) for i in range(NL, NA)]
            msg = sb("msg", [P, NB, T, P], stack=first)
            wt = [sb(f"wt{i}", [P, T, BLK], stack=first) for i in range(NX)]
            other = [sb(f"other{i}", [P, T, BLK], stack=first) for i in range(NO)]
        tan_hi = sb("tan_hi", [P, NB, T, P], f32r)
        tan_lo = sb("tan_lo", [P, NB, T, P], f32r)
        pair_hi = [sb(f"pair_hi{i}", [P, T, BLK], f32r) for i in range(NS)]
        pair_lo = [sb(f"pair_lo{i}", [P, T, BLK], f32r) for i in range(NS)]

        acc0 = [pb(f"acc0_{i}", [P, BLK]) for i in range(2)]
        acc1 = [pb(f"acc1_{i}", [P, BLK]) for i in range(2)]
        acc2 = pb("acc2", [P, BLK])
        turned = pb("turned", [P, T, P])
        mx_ps = pb("mx_ps", [P, 2, BLK])
        mx_out = mx_ps[:, :, 0:2 * (P + 1)].rearrange("p k (t f) -> p k t f", t=2)

        small_loaded = sem("small_loaded")
        eye_loaded = sem("eye_loaded")
        xcol_loaded = [sem(f"xcol_loaded{i}") for i in range(4)]
        adj_loaded = [sem(f"adj_loaded{i}") for i in range(NA)]
        other_loaded = [sem(f"other_loaded{i}") for i in range(NO)]
        xin_loaded = sem("xin_loaded")
        part_stored = sem("part_stored")
        own_loaded = sem("own_loaded")
        part_loaded = [sem(f"part_loaded{i}") for i in range(2)]
        zero_ready = sem("zero_ready")
        x1_stored = sem("x1_stored")
        out_stored = sem("out_stored")
        bias_sq = sem("bias_sq")
        bias_exp = sem("bias_exp")
        hb_ready = sem("hb_ready")
        hb_turned = sem("hb_turned")
        hbcol_ready = sem("hbcol_ready")
        wb_done = sem("wb_done")
        wb_ready = sem("wb_ready")
        msg_done = sem("msg_done")
        msg_ready = sem("msg_ready")
        ln_ready = sem("ln_ready")
        inv_ready = sem("inv_ready")
        z_ready = sem("z_ready")
        e_ready = sem("e_ready")
        w_ready = sem("w_ready")
        l0_done = sem("l0_done")
        other_done = sem("other_done")
        extra_ready = sem("extra_ready")
        part_ready = sem("part_ready")
        tan_hi_ready = sem("tan_hi_ready")
        tan_lo_ready = sem("tan_lo_ready")
        hi_ready = sem("hi_ready")
        lo_ready = sem("lo_ready")
        half_done = sem("half_done")
        late_done = sem("late_done")
        row_done = sem("row_done")
        act_ln = sem("act_ln")
        dve_step = sem("dve_step")
        act_step = sem("act_step")
        o_ready = sem("o_ready")
        o_turned = sem("o_turned")
        var_ready = sem("var_ready")
        rstd_ready = sem("rstd_ready")
        x1_ready = sem("x1_ready")
        x1_turned = sem("x1_turned")
        x1t_ready = sem("x1t_ready")
        mx_done = sem("mx_done")
        norms_ready = sem("norms_ready")
        roots_ready = sem("roots_ready")
        clip_ready = sem("clip_ready")
        art_ready = sem("art_ready")
        arg_ready = sem("arg_ready")
        tanh_ready = sem("tanh_ready")
        sum_ready = sem("sum_ready")
        sumroot_ready = sem("sumroot_ready")
        sumclip_ready = sem("sumclip_ready")
        sumart_ready = sem("sumart_ready")
        tan_ready = sem("tan_ready")
        y_o_ready = sem("y_o_ready")
        y_o_turned = sem("y_o_turned")
        relu_ready = sem("relu_ready")
        y_sq_ready = sem("y_sq_ready")
        relu_sq_ready = sem("relu_sq_ready")
        y_dev_ready = sem("y_dev_ready")
        dev_sq_ready = sem("dev_sq_ready")
        y_norms_ready = sem("y_norms_ready")
        y_roots_ready = sem("y_roots_ready")
        y_arg_ready = sem("y_arg_ready")
        y_tanh_ready = sem("y_tanh_ready")
        y_var_ready = sem("y_var_ready")
        y_rstd_ready = sem("y_rstd_ready")
        y_ready = sem("y_ready")
        y_xin_loaded = sem("y_xin_loaded")

        block = ctx.enter_context(nc.Block())

        def q(k, n=1):
            return s[:, k:k + n, :]

        def wide(k):
            return s[:, k, :].unsqueeze(2).to_broadcast([P, T, P])

        def late_count(m):
            r = LATE[m][0]
            if m + 1 == len(LATE) or LATE[m + 1][0] != r:
                return row_done, r + 1
            return late_done, m + 1 - r

        def half_count(j, half):
            return (half_done, j + 1) if half == 0 else late_count(SPLIT[j])

        def late_loaded(m):
            return (NB * NB // NA + m // NL + 1) * 16

        def due(slot, after):
            return [(r, k) for r in range(NB) for k, n in enumerate(after) if LAND_FROM[r] + n == slot]

        @block.sync
        def _(sp):
            def load(i, b):
                k = b % NA
                sp.dma_start(pair[k][:, :, :], adj[i, b]).then_inc(adj_loaded[k], 16)

            load(0, 0)
            for dst, src in ((w0_sb, w0), (b0_sb, b0), (b1_sb, b1)):
                sp.dma_start(dst, src).then_inc(small_loaded, 16)
            for i in range(4):
                cols = slice(i * N // 4, (i + 1) * N // 4)
                sp.dma_start(x_col[:, cols], x_cols[:, cols]).then_inc(xcol_loaded[i], 16)
                if i == 0:
                    for dst, src in ((w1_sb, w1), (w1c_sb[:, 0:P], w1_cols), (eye_sb[:, :], eye),
                                     (center_sb[:, :], center)):
                        sp.dma_start(dst, src).then_inc(eye_loaded, 16)
                if i < 3:
                    load(0, i + 1)

            def freed(n):
                sp.wait_ge(l0_done, n - NA + 2)

            before = {}
            for j, (i, at, r, b) in enumerate(OTHERS):
                before.setdefault(min(i * NB + at + 2, NB * NB - 1), []).append((j, r, b))
            for n in range(4, NB * NB):
                for j, r, b in before.get(n, []):
                    if j >= NO:
                        sp.wait_ge(other_done, j - NO + 1)
                    sp.dma_start(other[j % NO][:, :, :], adj[r, b]).then_inc(other_loaded[j % NO], 16)
                if n >= NA:
                    freed(n)
                load(n // NB, n % NB)
            for m, (r, b) in enumerate(LATE):
                if m < NL:
                    sp.wait_ge(l0_done, min(NB * NB + m - NA + 2, NB * NB))
                else:
                    sem_, value = late_count(m - NL)
                    sp.wait_ge(sem_, value)
                sp.dma_start(pair[m % NL][:, :, :], adj[r, b]).then_inc(adj_loaded[m % NL], 16)

        @block.gpsimd
        def _(pool):
            pool.dma_start(x_in[:, :, :], x_blocks[0]).then_inc(xin_loaded, 16)

            pool.wait_ge(zero_ready, 1)
            for r in range(2):
                pool.dma_start(part_dram[r], part[:, r, :]).then_inc(part_stored, 16)
            pool.wait_ge(part_stored, 2 * 16)

            def store_sums(i):
                pool.wait_ge(part_ready, i - 1)
                pool.dma_start(part_dram[i], part[:, 0, :]).then_inc(part_stored, 16)
                if OTHER[i]:
                    pool.dma_start(part_dram[i - 3], part[:, 1, :]).then_inc(part_stored, 16)
                stored = 2 + sum(1 for k in range(2, i + 1)) + sum(1 for k in range(i + 1) if OTHER[k])
                pool.wait_ge(part_stored, stored * 16)
                if i + 1 < NB:
                    pool.dma_start(part[:, 1, :], part_dram[i - 2]).then_inc(own_loaded, 16)

            def store_x1(i):
                pool.wait_ge(x1_ready, i + 1)
                pool.dma_start(x1_blocks[i], row[:, :, :]).then_inc(x1_stored, 16)
                pool.wait_ge(x1_stored, (i + 1) * 16)

            for i in range(NB):
                if OWN[i]:
                    store_sums(i)
                store_x1(i)
                if i + 1 < NB:
                    pool.dma_start(x_in[:, :, :], x_blocks[i + 1]).then_inc(xin_loaded, 16)
            pool.dma_start(x_in[:, :, :], x1_blocks[0]).then_inc(y_xin_loaded, 16)

            def load_sums(i):
                pool.dma_start(part[:, i % 2, :], part_dram[i]).then_inc(part_loaded[i % 2], 16)

            load_sums(0)
            load_sums(1)
            for i in range(NB):
                if i + 2 < NB:
                    pool.wait_ge(y_o_ready, i + 1)
                    load_sums(i + 2)
                if i + 1 < NB:
                    pool.wait_ge(y_dev_ready, i + 1)
                    pool.dma_start(x_in[:, :, :], x1_blocks[i + 1]).then_inc(y_xin_loaded, 16)
                pool.wait_ge(y_ready, i + 1)
                pool.dma_start(out_blocks[i], row[:, :, :]).then_inc(out_stored, 16)
            pool.wait_ge(out_stored, NB * 16)

        @block.scalar
        def _(act):
            nc.scalar.preload_act_table_set("natural_log_exp_and_others")

            def chained(ins, count):
                ins.then_inc(act_step, 1)
                act.wait_ge(act_step, count)

            act.wait_ge(bias_sq, 1)
            chained(nc.scalar.activation(c[:, 1:2], c[:, 0:1], ACT.Ln), 1)
            nc.scalar.activation(c[:, 2:3], c[:, 1:2], ACT.Exp, scale=-0.5)
            chained(nc.scalar.activation(c[:, 3:4], c[:, 1:2], ACT.Exp, scale=0.5), 2)
            nc.scalar.activation(c[:, 4:5], c[:, 3:4], ACT.Exp, scale=-2.0).then_inc(bias_exp, 1)

            def logs(i, b):
                k = b % NA
                act.wait_ge(adj_loaded[k], (i * (NB // NA) + (b // NA + 1)) * 16)
                if not (isinstance(i, int) and i * NB + b < NX):
                    act.wait_ge(l0_done, i * NB + (b - NX + 1))
                nc.scalar.activation(wt[b % NX][:, :, :], pair[k][:, :, :], ACT.Ln,
                                     bias=TINY_R).then_inc(ln_ready, 1)

            def inverses(i, b):
                act.wait_ge(ln_ready, i * NB + (b + 1))
                nc.scalar.activation(wt[b % NX][:, :, :], wt[b % NX][:, :, :], ACT.Exp,
                                     scale=-2.0).then_inc(inv_ready, 1)

            def exps(i, b):
                act.wait_ge(z_ready, i * NB + (b + 1))
                nc.scalar.activation(wt[b % NX][:, :, :], wt[b % NX][:, :, :], ACT.Exp,
                                     bias=-2.0, scale=4.0).then_inc(e_ready, 1)

            def lift(i, b):
                if b == 4:
                    act.wait_ge(var_ready, i + 1)
                    chained(nc.scalar.activation(q(1), q(0), ACT.Ln, scale=1.0 / P, bias=LN_EPS), i * 2 + 3)
                    nc.scalar.activation(q(2), q(1), ACT.Exp, scale=-0.5).then_inc(rstd_ready, 1)
                if b == 10:
                    act.wait_ge(norms_ready, i + 1)
                    chained(nc.scalar.activation(q(6, 2), q(4, 2), ACT.Ln), i * 2 + 4)
                    nc.scalar.activation(q(8), q(6), ACT.Exp, scale=0.5)
                    nc.scalar.activation(q(9), q(7), ACT.Exp, scale=-0.5).then_inc(roots_ready, 1)
                if b == 11:
                    act.wait_ge(clip_ready, i + 1)
                    nc.scalar.activation(q(12), q(10), ACT.Ln, bias=1.0)
                    nc.scalar.activation(q(13), q(10), ACT.Ln, scale=-1.0, bias=1.0)
                    nc.scalar.activation(q(14), q(11), ACT.Exp, scale=0.5).then_inc(art_ready, 1)
                if b == 12:
                    act.wait_ge(arg_ready, i + 1)
                    nc.scalar.activation(q(16), q(15), ACT.Exp, scale=-1.0).then_inc(tanh_ready, 1)
                if b == 14:
                    act.wait_ge(sum_ready, i + 1)
                    nc.scalar.activation(q(24), q(23), ACT.Ln, scale=-1.0, bias=1.0).then_inc(act_ln, 1)
                    act.wait_ge(act_ln, i + 1)
                    nc.scalar.activation(q(25), q(24), ACT.Exp, scale=0.5)
                    nc.scalar.activation(q(26), q(24), ACT.Exp, scale=-0.5)
                    nc.scalar.activation(q(29), q(22), ACT.Ln).then_inc(sumroot_ready, 1)
                if b == 15:
                    act.wait_ge(sumclip_ready, i + 1)
                    nc.scalar.activation(q(28), q(27), ACT.Ln, bias=1.0).then_inc(sumart_ready, 1)

            def step(i, first=False, last=False):
                for b in range(NB):
                    more = not (last and b + 1 >= NB)
                    if more:
                        logs(i, b + 1)
                    if not first:
                        lift(i - 1, b)
                    if more:
                        inverses(i, b + 1)
                    exps(i, b)

            logs(0, 0)
            inverses(0, 0)
            step(0, first=True)
            with act.Fori(1, NB - 1) as i:
                step(i)
            step(NB - 1, last=True)

            def split_tan(b):
                act.wait_ge(tan_ready, b + 1)
                nc.scalar.activation(tan_hi[:, b, :, :], tan[:, b, :, :], ACT.Copy).then_inc(tan_hi_ready, 1)

            def split(m, u):
                j = SPLIT.index(m)
                act.wait_ge(adj_loaded[m % NL], late_loaded(m))
                if j >= NS:
                    act.wait_ge(*half_count(j - NS, u))
                nc.scalar.activation(pair_hi[j % NS][:, HALVES[u], :], pair[m % NL][:, HALVES[u], :],
                                     ACT.Copy).then_inc(hi_ready, 1)

            act.wait_ge(l0_done, NB * NB)
            for b in range(NB):
                lift(NB - 1, b)
                if b < NB - 1:
                    split_tan(b)
            split_tan(NB - 1)

            def land(i, stage):
                if stage == 0:
                    if i > 0:
                        act.wait_ge(y_var_ready, i)
                    act.wait_ge(y_o_turned, i + 1)
                    nc.scalar.activation(x1_t[:, :, :], turned[:, :, :], ACT.Relu).then_inc(relu_ready, 1)
                    nc.scalar.activation(sq[:, :, :], turned[:, :, :], ACT.Square).then_inc(y_sq_ready, 1)
                    act.wait_ge(relu_ready, i + 1)
                    nc.scalar.activation(mx[:, :, :], x1_t[:, :, :], ACT.Square).then_inc(relu_sq_ready, 1)
                if stage == 1:
                    act.wait_ge(y_norms_ready, i + 1)
                    chained(nc.scalar.activation(q(6, 2), q(4, 2), ACT.Ln), i * 2 + 3 + 2 * NB)
                    nc.scalar.activation(q(8), q(6), ACT.Exp, scale=0.5)
                    nc.scalar.activation(q(9), q(6), ACT.Exp, scale=-0.5)
                    nc.scalar.activation(q(10), q(7), ACT.Exp, scale=0.5)
                    nc.scalar.activation(q(11), q(7), ACT.Exp, scale=-0.5).then_inc(y_roots_ready, 1)
                if stage == 2:
                    act.wait_ge(y_arg_ready, i + 1)
                    nc.scalar.activation(q(13), q(12), ACT.Exp, scale=-2.0).then_inc(y_tanh_ready, 1)
                if stage == 3:
                    act.wait_ge(y_dev_ready, i + 1)
                    nc.scalar.activation(sq[:, :, :], row[:, :, :], ACT.Square).then_inc(dev_sq_ready, 1)
                if stage == 4:
                    act.wait_ge(y_var_ready, i + 1)
                    chained(nc.scalar.activation(q(1), q(0), ACT.Ln, scale=1.0 / P, bias=LN_EPS),
                            i * 2 + 4 + 2 * NB)
                    nc.scalar.activation(q(2), q(1), ACT.Exp, scale=-0.5).then_inc(y_rstd_ready, 1)

            for slot in range(SLOTS + 1):
                if slot // 2 in SPLIT:
                    split(slot // 2, slot % 2)
                for r, stage in due(slot, LAND_SCALAR):
                    land(r, stage)

        @block.vector
        def _(dve):
            v = nc.vector
            state = {"base": 0, "count": 0}

            def mark(ins):
                state["count"] += 1
                ins.then_inc(dve_step, 1)

            def after_mark():
                dve.wait_ge(dve_step, state["base"] + state["count"])

            def link(ins):
                mark(ins)
                after_mark()

            def links(base, count, body):
                state["base"], state["count"] = base, 0
                body()
                assert state["count"] == count, state["count"]

            def pre():
                v.memset(part[:, :, :], 0.0).then_inc(zero_ready, 1)
                dve.wait_ge(small_loaded, 48)
                link(v.tensor_tensor(hb[:, :], b1_sb, b1_sb, ALU.mult))
                link(v.tensor_reduce(c[:, 5:6], hb[:, :], AX, ALU.add))
                v.tensor_scalar(c[:, 0:1], c[:, 5:6], MIN_NORM2, None, ALU.max).then_inc(bias_sq, 1)
                dve.wait_ge(bias_exp, 1)
                v.tensor_scalar(c[:, 6:7], c[:, 4:5], -1.0, 1.0, ALU.mult, ALU.add)
                link(v.tensor_scalar(c[:, 7:8], c[:, 4:5], 1.0, None, ALU.add))
                link(v.reciprocal(c[:, 8:9], c[:, 7:8]))
                link(v.tensor_scalar(c[:, 9:10], c[:, 6:7], c[:, 8:9], BALL, ALU.mult, ALU.min))
                v.tensor_scalar(hb[:, :], b1_sb, c[:, 9:10], c[:, 2:3], ALU.mult, ALU.mult).then_inc(hb_ready, 1)
                v.tensor_scalar(c[:, 5:6], c[:, 9:10], -1.0, 1.0, ALU.mult, ALU.add)
                link(v.tensor_tensor(c[:, 10:11], c[:, 9:10], c[:, 9:10], ALU.mult))
                v.tensor_scalar(c[:, 11:12], c[:, 10:11], 1.0, None, ALU.add)
                v.tensor_scalar(c[:, 12:13], c[:, 10:11], -1.0, None, ALU.mult)
                link(v.tensor_scalar(c[:, 6:7], c[:, 9:10], 1.0, None, ALU.add))
                link(v.tensor_tensor(c[:, 3:4], c[:, 5:6], c[:, 6:7], ALU.mult))
                dve.wait_ge(hb_turned, 1)
                v.tensor_copy(hb_col[:, :], turned[:, 0, 0:1]).then_inc(hbcol_ready, 1)
                dve.wait_ge(wb_done, 1)
                v.tensor_copy(w1c_sb[:, P:P + 1], mx_ps[:, 0, 0:1]).then_inc(wb_ready, 1)

            links(0, PRE_LINKS, pre)

            def messages(b):
                dve.wait_ge(msg_done, b + 1)
                v.tensor_tensor(msg[:, b, :, :], acc1[b % 2][:, :].rearrange("p (t f) -> p t f", t=T),
                                b0_sb.unsqueeze(1).to_broadcast([P, T, P]), ALU.add).then_inc(msg_ready, 1)

            def halves(i, b):
                buf = wt[b % NX][:, :, :]
                dve.wait_ge(inv_ready, i * NB + (b + 1))
                v.scalar_tensor_tensor(buf, pair[b % NA][:, :, :], 0.5, buf, ALU.subtract, ALU.mult).then_inc(z_ready, 1)

            def masks(i, b):
                buf = wt[b % NX][:, :, :]
                dve.wait_ge(e_ready, i * NB + (b + 1))
                v.scalar_tensor_tensor(buf, pair[b % NA][:, :, :], 1.0, buf, ALU.is_lt, ALU.mult).then_inc(w_ready, 1)

            def refined_rstd():
                v.tensor_scalar(q(30), q(0), 1.0 / P, LN_EPS, ALU.mult, ALU.add)
                link(v.scalar_tensor_tensor(q(31), q(2), -0.5, q(2), ALU.mult, ALU.mult))
                link(v.tensor_tensor(q(30), q(30), q(31), ALU.mult))
                link(v.scalar_tensor_tensor(q(3), q(30), 1.5, q(2), ALU.add, ALU.mult))

            def lift(i, k, early_sums=2):
                if k == 1:
                    dve.wait_ge(l0_done, (i + 1) * NB)
                    dve.wait_ge(xin_loaded, (i + 1) * 16)
                    v.tensor_tensor(o_t[:, :, :].rearrange("p t f -> p (t f)"), acc0[lift_marks["acc"]][:, :],
                                    x_in[:, :, :].rearrange("p t f -> p (t f)"), ALU.add).then_inc(o_ready, 1)
                if k == 2:
                    if early_sums >= 1:
                        dve.wait_ge(*((own_loaded, (i - 2) * 16) if early_sums > 1 else (part_stored, 2 * 16)))
                        ins = v.tensor_copy(part[:, 0, :], acc1[lift_marks["acc"]][:, :])
                        if early_sums == 2 or (early_sums == 3 and OTHER[NB - 1]):
                            ins = v.tensor_tensor(part[:, 1, :], acc2[:, :], part[:, 1, :], ALU.add)
                        ins.then_inc(part_ready, 1)
                if k == 4:
                    dve.wait_ge(o_turned, i + 1)
                    mark(v.tensor_copy(row[:, :, :], turned[:, :, :]))
                if k == 5:
                    after_mark()
                    mark(v.tensor_tensor(sq[:, :, :], row[:, :, :], row[:, :, :], ALU.mult))
                if k == 6:
                    after_mark()
                    v.tensor_reduce(q(0), sq[:, :, :], AX, ALU.add).then_inc(var_ready, 1)
                if k == 8:
                    dve.wait_ge(rstd_ready, i + 1)
                    v.tensor_scalar(q(30), q(0), 1.0 / P, LN_EPS, ALU.mult, ALU.add)
                    mark(v.scalar_tensor_tensor(q(31), q(2), -0.5, q(2), ALU.mult, ALU.mult))
                if k == 9:
                    after_mark()
                    link(v.tensor_tensor(q(30), q(30), q(31), ALU.mult))
                    mark(v.scalar_tensor_tensor(q(3), q(30), 1.5, q(2), ALU.add, ALU.mult))
                if k == 10:
                    after_mark()
                    v.tensor_tensor(row[:, :, :], row[:, :, :], wide(3), ALU.mult).then_inc(x1_ready, 1)
                    mark(v.tensor_tensor(q(30), q(0), q(3), ALU.mult))
                if k == 11:
                    after_mark()
                    link(v.tensor_tensor(q(31), q(30), q(3), ALU.mult))
                    v.tensor_scalar(q(4), q(31), MIN_NORM2, None, ALU.max)
                if k == 13:
                    dve.wait_ge(x1_turned, i + 1)
                    v.tensor_copy(x1_t[:, :, :], turned[:, :, :]).then_inc(x1t_ready, 1)
                if k == 15:
                    dve.wait_ge(mx_done, i + 1)
                    v.tensor_copy(s[:, 17, :].rearrange("p (k t) -> p k t", k=2), mx_out[:, :, :, P])
                    mark(v.tensor_copy(mx[:, :, :].rearrange("p (k t) f -> p k t f", k=2), mx_out[:, :, :, 0:P]))
                if k == 16:
                    after_mark()
                    mark(v.tensor_tensor(sq[:, :, :], mx[:, :, :], mx[:, :, :], ALU.mult))
                if k == 17:
                    after_mark()
                    mark(v.tensor_reduce(q(31), sq[:, :, :], AX, ALU.add))
                if k == 18:
                    after_mark()
                    v.tensor_scalar(q(5), q(31), MIN_NORM2, None, ALU.max).then_inc(norms_ready, 1)
                if k == 20:
                    dve.wait_ge(roots_ready, i + 1)
                    v.tensor_scalar(q(10), q(8), ART_MAX, None, ALU.min)
                    v.tensor_tensor(q(11), q(7), q(6), ALU.subtract).then_inc(clip_ready, 1)
                if k == 22:
                    dve.wait_ge(art_ready, i + 1)
                    link(v.tensor_tensor(q(15), q(12), q(13), ALU.subtract))
                    v.tensor_tensor(q(15), q(15), q(14), ALU.mult).then_inc(arg_ready, 1)
                if k == 24:
                    dve.wait_ge(tanh_ready, i + 1)
                    v.tensor_scalar(q(18), q(16), EXP_BALL, None, ALU.max)
                    link(v.tensor_scalar(q(19), q(16), EXP_BALL, 1.0, ALU.max, ALU.add))
                    link(v.reciprocal(q(20), q(19)))
                    v.tensor_scalar(q(19), q(20), 2.0, -1.0, ALU.mult, ALU.add)
                    mark(v.tensor_tensor(q(21), q(18), q(20), ALU.mult))
                if k == 25:
                    after_mark()
                    v.scalar_tensor_tensor(q(18), q(21), 4.0, q(20), ALU.mult, ALU.mult)
                    link(v.tensor_tensor(q(19), q(19), q(9), ALU.mult))
                    link(v.tensor_tensor(q(17), q(17), q(19), ALU.mult))
                    link(v.tensor_scalar(q(21), q(17), 2.0, c[:, 11:12], ALU.mult, ALU.add))
                    mark(v.scalar_tensor_tensor(q(31), q(18), c[:, 12:13], q(21), ALU.mult, ALU.add))
                if k == 26:
                    after_mark()
                    v.tensor_tensor(q(21), q(21), q(19), ALU.mult)
                    link(v.tensor_scalar(q(31), q(31), 1e-15, None, ALU.max))
                    link(v.reciprocal(q(30), q(31)))
                    link(v.scalar_tensor_tensor(q(31), q(18), c[:, 3:4], q(30), ALU.mult, ALU.mult))
                    v.tensor_scalar(q(22), q(31), BALL_GAP, P_MAX, ALU.max, ALU.min)
                    v.tensor_scalar(q(23), q(31), P_MAX, None, ALU.min).then_inc(sum_ready, 1)
                if k == 28:
                    dve.wait_ge(sumroot_ready, i + 1)
                    v.tensor_scalar(q(27), q(25), BALL, None, ALU.min).then_inc(sumclip_ready, 1)
                    mark(v.tensor_tensor(q(24), q(26), q(30), ALU.mult))
                if k == 30:
                    dve.wait_ge(sumart_ready, i + 1)
                    after_mark()
                    link(v.scalar_tensor_tensor(q(31), q(29), -0.5, q(28), ALU.mult, ALU.add))
                    link(v.tensor_tensor(q(31), q(31), q(24), ALU.mult))
                    v.tensor_tensor(q(23), q(18), q(31), ALU.mult)
                    mark(v.tensor_tensor(q(22), q(21), q(31), ALU.mult))
                if k == 31:
                    after_mark()
                    hb_wide = hb[:, :].unsqueeze(1).to_broadcast([P, T, P])
                    v.tensor_tensor(mx[:, :, :], mx[:, :, :], wide(22), ALU.mult)
                    link(v.tensor_tensor(sq[:, :, :], hb_wide, wide(23), ALU.mult))
                    v.tensor_tensor(tan[:, i, :, :], mx[:, :, :], sq[:, :, :], ALU.add).then_inc(tan_ready, 1)

            lift_marks = {"acc": None}

            def keep_extra(i, odd):
                dve.wait_ge(other_done, max(j for j, (k, _, r, _) in enumerate(OTHERS)
                                            if (k, r) == (i, EXTRA_ROW[i])) + 1)
                kept = extra[:, EXTRA_ROW[i] - (NB - 2), :]
                if EXTRA_ROW[i] in [EXTRA_ROW[k] for k in EXTRA_ROW if k < i]:
                    dve.wait_ge(extra_ready, list(EXTRA_ROW).index(i))
                    ins = v.tensor_tensor(kept, acc1[1 - odd][:, :], kept, ALU.add)
                else:
                    ins = v.tensor_copy(kept, acc1[1 - odd][:, :])
                ins.then_inc(extra_ready, 1)

            def step(i, odd, first=False, last=False, early_sums=2):
                lift_marks["acc"] = 1 - odd

                def body():
                    for b in range(NB):
                        if first:
                            messages(b)
                        if not (last and b + 1 >= NB):
                            halves(i, b + 1)
                        if not first:
                            lift(i - 1, 2 * b, early_sums)
                        masks(i, b)
                        if not first:
                            lift(i - 1, 2 * b + 1, early_sums)
                    if isinstance(i, int) and i in EXTRA_ROW:
                        keep_extra(i, odd)

                links(PRE_LINKS + (i - 1) * LIFT_LINKS, 0 if first else LIFT_LINKS, body)

            halves(0, 0)
            step(0, 0, first=True)
            step(1, 1, early_sums=0)
            step(2, 0, early_sums=0)
            step(3, 1, early_sums=1)
            step(4, 0)
            step(5, 1)
            step(6, 0)
            with dve.Fori(7, NB - 1, 2) as i:
                step(i, 1)
                step(i + 1, 0)
            step(NB - 1, 1, last=True)
            lift_marks["acc"] = 1

            def split_tan(b):
                dve.wait_ge(tan_hi_ready, b + 1)
                v.tensor_tensor(tan_lo[:, b, :, :], tan[:, b, :, :], tan_hi[:, b, :, :].bitcast(f32),
                                ALU.subtract).then_inc(tan_lo_ready, 1)

            def split(m, u):
                j = SPLIT.index(m)
                dve.wait_ge(hi_ready, 2 * j + u + 1)
                v.tensor_tensor(pair_lo[j % NS][:, HALVES[u], :], pair[m % NL][:, HALVES[u], :],
                                pair_hi[j % NS][:, HALVES[u], :].bitcast(f32), ALU.subtract).then_inc(lo_ready, 1)

            def last_lift():
                for k in range(2 * NB):
                    lift(NB - 1, k, early_sums=3)
                    if k % 2 == 1 and k // 2 < NB - 1:
                        split_tan(k // 2)

            links(PRE_LINKS + (NB - 1) * LIFT_LINKS, LIFT_LINKS, last_lift)
            split_tan(NB - 1)

            def land(i, stage):
                o_flat = o_t[:, :, :].rearrange("p t f -> p (t f)")
                if stage == 0:
                    dve.wait_ge(row_done, i + 1)
                    dve.wait_ge(part_loaded[i % 2], (i // 2 + 1) * 16)
                    if i >= NB - 2:
                        link(v.tensor_tensor(o_flat, acc1[i % 2][:, :], extra[:, i - (NB - 2), :], ALU.add))
                        v.tensor_tensor(o_flat, o_flat, part[:, i % 2, :], ALU.add).then_inc(y_o_ready, 1)
                    else:
                        v.tensor_tensor(o_flat, acc1[i % 2][:, :], part[:, i % 2, :], ALU.add).then_inc(y_o_ready, 1)
                if stage == 1:
                    dve.wait_ge(y_sq_ready, i + 1)
                    v.tensor_reduce(q(30), sq[:, :, :], AX, ALU.add)
                    dve.wait_ge(relu_sq_ready, i + 1)
                    mark(v.tensor_reduce(q(31), mx[:, :, :], AX, ALU.add))
                if stage == 2:
                    after_mark()
                    v.tensor_scalar(q(4, 2), q(30, 2), MIN_NORM2, None, ALU.max).then_inc(y_norms_ready, 1)
                if stage == 3:
                    dve.wait_ge(y_roots_ready, i + 1)
                    link(v.tensor_scalar(q(12), q(8), ART_BALL, None, ALU.min))
                    link(v.tensor_tensor(q(14), q(12), q(9), ALU.mult))
                    v.tensor_tensor(q(12), q(14), q(10), ALU.mult).then_inc(y_arg_ready, 1)
                if stage == 4:
                    dve.wait_ge(y_tanh_ready, i + 1)
                    v.tensor_scalar(q(15), q(13), -1.0, 1.0, ALU.mult, ALU.add)
                    link(v.tensor_scalar(q(16), q(13), 1.0, None, ALU.add))
                    mark(v.reciprocal(q(17), q(16)))
                if stage == 5:
                    after_mark()
                    link(v.tensor_tensor(q(15), q(15), q(17), ALU.mult))
                    link(v.tensor_scalar(q(15), q(15), BALL, None, ALU.min))
                    mark(v.tensor_tensor(q(18), q(15), q(11), ALU.mult))
                if stage == 6:
                    after_mark()
                    link(v.tensor_tensor(x1_t[:, :, :], x1_t[:, :, :], wide(18), ALU.mult))
                    dve.wait_ge(y_xin_loaded, (i + 1) * 16)
                    if i > 0:
                        dve.wait_ge(out_stored, i * 16)
                    mark(v.tensor_tensor(row[:, :, :], x1_t[:, :, :], x_in[:, :, :], ALU.add))
                if stage == 7:
                    after_mark()
                    link(v.tensor_reduce(q(3), row[:, :, :], AX, ALU.add))
                    mark(v.tensor_scalar(q(1), q(3), -1.0 / P, None, ALU.mult))
                if stage == 8:
                    after_mark()
                    v.tensor_tensor(row[:, :, :], row[:, :, :], wide(1), ALU.add).then_inc(y_dev_ready, 1)
                if stage == 9:
                    dve.wait_ge(dev_sq_ready, i + 1)
                    v.tensor_reduce(q(0), sq[:, :, :], AX, ALU.add).then_inc(y_var_ready, 1)
                if stage == 10:
                    dve.wait_ge(y_rstd_ready, i + 1)
                    refined_rstd()
                if stage == 11:
                    v.tensor_tensor(row[:, :, :], row[:, :, :], wide(3), ALU.mult).then_inc(y_ready, 1)

            state["base"], state["count"] = PRE_LINKS + NB * LIFT_LINKS, 0
            for slot in range(SLOTS + 1):
                if slot // 2 in SPLIT:
                    split(slot // 2, slot % 2)
                for r, stage in due(slot, LAND_VECTOR):
                    land(r, stage)

        @block.tensor
        def _(pe):
            mm = nc.tensor.matmul

            pe.wait_ge(eye_loaded, 64)
            pe.wait_ge(hb_ready, 1)
            nc.tensor.transpose(turned[:, 0, :], hb[:, :], eye_sb[:, :]).then_inc(hb_turned, 1)
            pe.wait_ge(hbcol_ready, 1)
            mm(mx_ps[:, 0, 0:1], w1_sb, hb_col[:, :], start=True, stop=True).then_inc(wb_done, 1)

            def messages(b):
                if b % 4 == 0:
                    pe.wait_ge(xcol_loaded[b // 4], 16)
                if b >= 2:
                    pe.wait_ge(msg_ready, b - 1)
                for t in range(T):
                    col = (b * T + t) * P
                    last = mm(acc1[b % 2][:, t * P:(t + 1) * P], x_col[:, col:col + P], w0_sb,
                              start=True, stop=True)
                last.then_inc(msg_done, 1)

            def layer0(i, b, odd, first):
                if first:
                    pe.wait_ge(msg_ready, b + 1)
                pe.wait_ge(w_ready, i * NB + (b + 1))
                for t in range(T):
                    last = mm(acc0[odd][:, :], msg[:, b, t, :], wt[b % NX][:, t, :],
                              start=(b == 0 and t == 0), stop=(b == NB - 1 and t == T - 1))
                last.then_inc(l0_done, 1)

            def lift(i, b):
                if b == 0:
                    pe.wait_ge(o_ready, i + 1)
                    for t in range(T):
                        last = mm(turned[:, t, :], o_t[:, t, :], center_sb[:, :], start=True, stop=True)
                    last.then_inc(o_turned, 1)
                if b == 5:
                    pe.wait_ge(x1_ready, i + 1)
                    for t in range(T):
                        last = nc.tensor.transpose(turned[:, t, :], row[:, t, :], eye_sb[:, :])
                    last.then_inc(x1_turned, 1)
                if b == 6:
                    pe.wait_ge(x1t_ready, i + 1)
                    for t in range(T):
                        last = mm(mx_out[:, t // 2, t % 2, :], x1_t[:, t, :], w1c_sb[:, :], start=True, stop=True)
                    last.then_inc(mx_done, 1)

            def own_layer1(i, b, odd):
                if b == OWN[i][0] and i - 1 in EXTRA_ROW:
                    pe.wait_ge(extra_ready, list(EXTRA_ROW).index(i - 1) + 1)
                for t in range(T):
                    mm(acc1[odd][:, :], tan[:, b, t, :], pair[b % NA][:, t, :],
                       start=(b == OWN[i][0] and t == 0), stop=(b == OWN[i][-1] and t == T - 1))

            def other_layer1(j):
                i, at, r, b = OTHERS[j]
                is_extra = i in EXTRA_ROW and r == EXTRA_ROW[i]
                jobs, acc = (EXTRA[i], acc1[1 - i % 2]) if is_extra else (OTHER[i], acc2)
                pe.wait_ge(other_loaded[j % NO], (j // NO + 1) * 16)
                if (at, b) == jobs[0] and i >= 4:
                    pe.wait_ge(part_ready, i - 2)
                for t in range(T):
                    last = mm(acc[:, :], tan[:, b, t, :], other[j % NO][:, t, :],
                              start=((at, b) == jobs[0] and t == 0), stop=((at, b) == jobs[-1] and t == T - 1))
                last.then_inc(other_done, 1)

            def step(i, odd, first=False):
                for b in range(NB):
                    if first and b + 2 < NB:
                        messages(b + 2)
                    if not first and b in (5, 6):
                        lift(i - 1, b)
                    layer0(i, b, odd, first)
                    if not first and b == 0:
                        lift(i - 1, b)
                    if b == 0 and i >= 2:
                        pe.wait_ge(tan_ready, i - 1)
                    if b in OWN[i]:
                        own_layer1(i, b, odd)
                    if (i, b) in other_at:
                        other_layer1(other_at[i, b])

            other_at = {(i, at): j for j, (i, at, _, _) in enumerate(OTHERS)}
            pe.wait_ge(small_loaded, 48)
            messages(0)
            messages(1)
            pe.wait_ge(wb_ready, 1)
            for i in range(NB):
                step(i, i % 2, first=(i == 0))

            def late_layer1(m):
                r, b = LATE[m]
                row = late_row(r)
                acc = acc1[r % 2][:, :]
                if m in SPLIT:
                    j = SPLIT.index(m)
                    pe.wait_ge(tan_lo_ready, b + 1)
                    for t in range(T):
                        if t % (T // 2) == 0:
                            pe.wait_ge(lo_ready, 2 * j + t // (T // 2) + 1)
                        hi, lo = tan_hi[:, b, t, :], tan_lo[:, b, t, :]
                        pair_h, pair_l = pair_hi[j % NS][:, t, :], pair_lo[j % NS][:, t, :]
                        mm(acc, hi, pair_h, start=(b == row[0] and t == 0), stop=False)
                        mm(acc, hi, pair_l, start=False, stop=False)
                        last = mm(acc, lo, pair_h, start=False, stop=(b == row[-1] and t == T - 1))
                        if t == T // 2 - 1:
                            last.then_inc(half_done, 1)
                else:
                    pe.wait_ge(adj_loaded[m % NL], late_loaded(m))
                    if r == 0:
                        pe.wait_ge(tan_ready, b + 1)
                    for t in range(T):
                        last = mm(acc, tan[:, b, t, :], pair[m % NL][:, t, :],
                                  start=(b == row[0] and t == 0), stop=(b == row[-1] and t == T - 1))
                last.then_inc(late_count(m)[0], 1)

            def land(i):
                pe.wait_ge(y_o_ready, i + 1)
                for t in range(T):
                    last = nc.tensor.transpose(turned[:, t, :], o_t[:, t, :], eye_sb[:, :])
                last.then_inc(y_o_turned, 1)

            for m, (r, b) in enumerate(LATE):
                late_layer1(m)
                if r == 0:
                    lift(NB - 1, m)
                elif 2 * m - LAND_TENSOR in LAND_FROM:
                    land(LAND_FROM.index(2 * m - LAND_TENSOR))
            for r in range(NB):
                if LAND_FROM[r] + LAND_TENSOR > 2 * (len(LATE) - 1):
                    land(r)


def kernel(x, adj, L0_gnn_W, L0_gnn_B, L1_gnn_weight, L1_gnn_bias):
    import concourse.bacc as bacc
    from concourse.bass_utils import run_bass_kernel_spmd

    x, adj = np.asarray(x), np.asarray(adj)
    w1 = np.asarray(L1_gnn_weight)
    arrays = {
        "x_cols": x.T,
        "adj": adj.reshape(NB, BLK, NB, T, P).transpose(0, 2, 4, 3, 1),
        "w0": np.asarray(L0_gnn_W),
        "b0": np.broadcast_to(np.asarray(L0_gnn_B), (P, P)),
        "w1": w1,
        "w1_cols": w1.T,
        "b1": np.broadcast_to(np.asarray(L1_gnn_bias), (P, P)),
        "eye": np.eye(P, dtype=np.float32),
        "center": np.eye(P, dtype=np.float32) - np.float32(1.0 / P),
    }
    arrays = {k: np.ascontiguousarray(a) for k, a in arrays.items()}
    nc = bacc.Bacc("TRN2", target_bir_lowering=False, num_devices=1)
    args = [nc.dram_tensor(f"in_{k}", a.shape, mybir.dt.from_np(a.dtype), kind="ExternalInput").ap()
            for k, a in arrays.items()]
    x1_dram = nc.dram_tensor("x1_rows", (N, P), mybir.dt.float32).ap()
    part_dram = nc.dram_tensor("early_sums", (NB, P, BLK), mybir.dt.float32).ap()
    out = nc.dram_tensor("out_y", (N, P), mybir.dt.float32, kind="ExternalOutput").ap()
    gnn_kernel(nc, *args, x1_dram, part_dram, out)
    r = run_bass_kernel_spmd(nc, [{f"in_{k}": a for k, a in arrays.items()}], core_ids=[0])
    return r.results[0]["out_y"]
```
